# Optimizing a Trainium2 kernel written in Bass

```python
import numpy as np
import jax
import jax.numpy as jnp

def _softmax(x, axis=-1):
    return jax.nn.softmax(x, axis=axis)

def _gelu(x):
    return jax.nn.gelu(x, approximate=True)

def _silu(x):
    return jax.nn.silu(x)

def _sigmoid(x):
    return jax.nn.sigmoid(x)

def _layernorm(x, axis=-1, eps=1e-05):
    m = jnp.mean(x, axis=axis, keepdims=True)
    v = jnp.var(x, axis=axis, keepdims=True)
    return (x - m) / jnp.sqrt(v + eps)

def _scatter_add(tgt, idx, src, axis=0):
    return tgt.at[idx].add(src)

def _segment_sum(src, seg, n):
    return jax.ops.segment_sum(src, seg, n)
kernel_name = 'mk_gnn_resnorm_d1_gnn_r32_9beb97'

def setup_inputs(seed: int=0):
    np.random.seed(seed)
    _w = jnp.asarray

    def _rec_inputs():
        import jax
        import jax.numpy as jnp
        _gk = jax.random.key(seed)
        x = -1.686e-05 + 1 * jax.random.normal(jax.random.fold_in(_gk, 1), (3125, 160), jnp.float32)
        _s = jax.random.randint(jax.random.fold_in(_gk, 2), (25000,), 0, 3125, jnp.int32)
        _d = jax.random.randint(jax.random.fold_in(_gk, 3), (25000,), 0, 3125, jnp.int32)
        _loop = jnp.arange(3125, dtype=jnp.int32)
        src = jnp.concatenate([_s, _d, _loop])
        dst = jnp.concatenate([_d, _s, _loop])
        _o = jnp.argsort(dst, stable=True)
        src = src[_o]
        dst = dst[_o]
        edge_attr_10 = jax.random.uniform(jax.random.fold_in(_gk, 12), (53125, 10), jnp.float32, 0.0, 1)
        edge_attr_4 = -0.000107899 + 1.00008 * jax.random.normal(jax.random.fold_in(_gk, 13), (53125, 4), jnp.float32)
        node_vec1 = jax.random.uniform(jax.random.fold_in(_gk, 14), (3125, 1), jnp.float32, 0.0, 1)
        return (x, src, dst, edge_attr_10, edge_attr_4, node_vec1)
    x, src, dst, edge_attr_10, edge_attr_4, node_vec1 = _rec_inputs()

    def _L0_gnn_setup():
        import jax, jax.numpy as jnp
        import numpy as np
        N_NODES = 50000
        N_EDGES = 25000
        MUL0, MUL1 = (64, 32)
        N_BASIS, N_RADIAL = (10, 100)
        W_NUMEL = 192
        NUM_NEIGHBORS = 16.0
        INV_SQRT3 = np.float32(1.0 / np.sqrt(3.0))
        RELU_GAIN = np.float32(np.sqrt(2.0))
        FAN_L2 = np.float32(np.sqrt(MUL0 + MUL1))

        def _fctp_scalar_attr(x0, x1, a, W0, W1):
            o0 = x0 @ W0 * a * (1.0 / np.sqrt(W0.shape[0]))
            o1 = jnp.einsum('nud,uw->nwd', x1, W1) * a[..., None] * (1.0 / np.sqrt(W1.shape[0]))
            return (o0, o1)
        key = jax.random.key(seed)
        ks = jax.random.split(key, 16)
        return {'node_input': jax.random.normal(ks[0], (N_NODES, MUL0 + 3 * MUL1), jnp.float32), 'node_attr': jnp.ones((N_NODES, 1), jnp.float32), 'edge_attr': jax.random.normal(ks[1], (N_EDGES, 4), jnp.float32), 'edge_length_embedded': jax.random.uniform(ks[2], (N_EDGES, N_BASIS), dtype=jnp.float32), 'W_si0': jax.random.normal(ks[3], (MUL0, MUL0), jnp.float32), 'W_si1': jax.random.normal(ks[4], (MUL1, MUL1), jnp.float32), 'W_l1_0': jax.random.normal(ks[5], (MUL0, MUL0), jnp.float32), 'W_l1_1': jax.random.normal(ks[6], (MUL1, MUL1), jnp.float32), 'W_l2_00': jax.random.normal(ks[7], (MUL0, MUL0), jnp.float32), 'W_l2_10': jax.random.normal(ks[8], (MUL1, MUL0), jnp.float32), 'W_l2_01': jax.random.normal(ks[9], (MUL0, MUL1), jnp.float32), 'W_l2_11': jax.random.normal(ks[10], (MUL1, MUL1), jnp.float32), 'W_fc1': jax.random.normal(ks[11], (N_BASIS, N_RADIAL), jnp.float32), 'W_fc2': jax.random.normal(ks[12], (N_RADIAL, W_NUMEL), jnp.float32), 'edge_src': jax.random.randint(ks[13], (N_EDGES,), 0, N_NODES), 'edge_dst': jax.random.randint(ks[14], (N_EDGES,), 0, N_NODES)}
    _L0_gnn_all = _L0_gnn_setup()
    _L0_gnn_in = {k: v for k, v in _L0_gnn_all.items() if k in ('W_si0', 'W_si1', 'W_l1_0', 'W_l1_1', 'W_l2_00', 'W_l2_10', 'W_l2_01', 'W_l2_11', 'W_fc1', 'W_fc2')}
    del _L0_gnn_all
    return {'x': x, 'src': src, 'dst': dst, 'edge_attr_10': edge_attr_10, 'edge_attr_4': edge_attr_4, 'node_vec1': node_vec1, 'L0_gnn_W_si0': _L0_gnn_in['W_si0'], 'L0_gnn_W_si1': _L0_gnn_in['W_si1'], 'L0_gnn_W_l1_0': _L0_gnn_in['W_l1_0'], 'L0_gnn_W_l1_1': _L0_gnn_in['W_l1_1'], 'L0_gnn_W_l2_00': _L0_gnn_in['W_l2_00'], 'L0_gnn_W_l2_10': _L0_gnn_in['W_l2_10'], 'L0_gnn_W_l2_01': _L0_gnn_in['W_l2_01'], 'L0_gnn_W_l2_11': _L0_gnn_in['W_l2_11'], 'L0_gnn_W_fc1': _L0_gnn_in['W_fc1'], 'L0_gnn_W_fc2': _L0_gnn_in['W_fc2']}

def reference(x, src, dst, edge_attr_10, edge_attr_4, node_vec1, L0_gnn_W_si0, L0_gnn_W_si1, L0_gnn_W_l1_0, L0_gnn_W_l1_1, L0_gnn_W_l2_00, L0_gnn_W_l2_10, L0_gnn_W_l2_01, L0_gnn_W_l2_11, L0_gnn_W_fc1, L0_gnn_W_fc2):
    import jax
    import jax.numpy as jnp

    def _L0_gnn_ref(node_input, node_attr, edge_src, edge_dst, edge_attr, edge_length_embedded, W_si0, W_si1, W_l1_0, W_l1_1, W_l2_00, W_l2_10, W_l2_01, W_l2_11, W_fc1, W_fc2):
        import jax, jax.numpy as jnp
        import numpy as np
        N_NODES = 50000
        N_EDGES = 25000
        MUL0, MUL1 = (64, 32)
        N_BASIS, N_RADIAL = (10, 100)
        W_NUMEL = 192
        NUM_NEIGHBORS = 16.0
        INV_SQRT3 = np.float32(1.0 / np.sqrt(3.0))
        RELU_GAIN = np.float32(np.sqrt(2.0))
        FAN_L2 = np.float32(np.sqrt(MUL0 + MUL1))

        def _fctp_scalar_attr(x0, x1, a, W0, W1):
            o0 = x0 @ W0 * a * (1.0 / np.sqrt(W0.shape[0]))
            o1 = jnp.einsum('nud,uw->nwd', x1, W1) * a[..., None] * (1.0 / np.sqrt(W1.shape[0]))
            return (o0, o1)
        N = node_input.shape[0]
        x0 = node_input[:, :MUL0]
        x1 = node_input[:, MUL0:].reshape(N, MUL1, 3)
        a = node_attr
        h = jax.nn.relu(edge_length_embedded @ W_fc1 * (1.0 / np.sqrt(N_BASIS))) * RELU_GAIN
        w = h @ W_fc2 * (1.0 / np.sqrt(N_RADIAL))
        w0, w1, w2, w3 = (w[:, :64], w[:, 64:128], w[:, 128:160], w[:, 160:192])
        si0, si1 = _fctp_scalar_attr(x0, x1, a, W_si0, W_si1)
        l0, l1 = _fctp_scalar_attr(x0, x1, a, W_l1_0, W_l1_1)
        y0 = l0[edge_src]
        y1 = l1[edge_src]
        e0 = edge_attr[:, :1]
        e1 = edge_attr[:, 1:4]
        m0 = w0 * y0 * e0
        m1 = (w1 * y0)[:, :, None] * e1[:, None, :]
        m2 = (w2 * e0)[:, :, None] * y1
        m3 = w3 * jnp.einsum('eud,ed->eu', y1, e1) * INV_SQRT3
        inv = np.float32(1.0 / np.sqrt(NUM_NEIGHBORS))
        s0 = jax.ops.segment_sum(m0, edge_dst, num_segments=N) * inv
        s1 = jax.ops.segment_sum(m1, edge_dst, num_segments=N) * inv
        s2 = jax.ops.segment_sum(m2, edge_dst, num_segments=N) * inv
        s3 = jax.ops.segment_sum(m3, edge_dst, num_segments=N) * inv
        o0 = (s0 @ W_l2_00 + s3 @ W_l2_10) * a / FAN_L2
        o1 = (jnp.einsum('nud,uw->nwd', s1, W_l2_01) + jnp.einsum('nud,uw->nwd', s2, W_l2_11)) * a[..., None] / FAN_L2
        out0 = si0 + 0.5 * o0
        out1 = si1 + 0.5 * o1
        return jnp.concatenate([out0, out1.reshape(N, 3 * MUL1)], axis=1)
    x = _layernorm(x + _L0_gnn_ref(x, node_vec1, src, dst, edge_attr_4, edge_attr_10, L0_gnn_W_si0, L0_gnn_W_si1, L0_gnn_W_l1_0, L0_gnn_W_l1_1, L0_gnn_W_l2_00, L0_gnn_W_l2_10, L0_gnn_W_l2_01, L0_gnn_W_l2_11, L0_gnn_W_fc1, L0_gnn_W_fc2), axis=-1)
    return x

_drawn_inputs = setup_inputs


def setup_inputs(seed=0):
    import zlib

    import numpy as np

    out = dict(_drawn_inputs(seed))
    spreads = {}
    factors = {}
    for name, (base, spread) in spreads.items():
        noise = np.random.default_rng([zlib.crc32(name.encode()), seed]).standard_normal(out[name].shape)
        drawn = base * np.exp(spread * noise) if base else spread * noise
        out[name] = jnp.asarray(drawn.astype(out[name].dtype))
    for name, factor in factors.items():
        out[name] = (out[name] * factor).astype(out[name].dtype)
    return out
```

```python
from contextlib import ExitStack

import numpy as np

import concourse.bass as bass
from concourse import mybir

F32 = mybir.dt.float32
I32 = mybir.dt.int32
ALU = mybir.AluOpType
ACT = mybir.ActivationFunctionType
AX = mybir.AxisListType

P = 128
BANK = 512
N_NODES, N_EDGES = 3125, 53125
MUL0, MUL1, DIMS = 64, 32, 3
VEC = MUL1 * DIMS
FEAT = MUL0 + VEC
N_BASIS, N_RADIAL = 10, 100
W_NUMEL = 2 * MUL0 + 2 * MUL1
BLOCKS = -(-N_NODES // P)
NPAD = BLOCKS * P

TILES = 4
GROUP = TILES * P
GROUPS = -(-N_EDGES // GROUP)
EPAD = GROUPS * GROUP
SLOTS = 4
TURNS_END = GROUPS - SLOTS + 1
WIN = 40
LAST_WIN = NPAD - WIN
PASSES = -(-N_NODES // WIN)
assert GROUPS % SLOTS == 0 and LAST_WIN >= N_NODES

C_W0Y0, C_W2Y1, C_W3Y1, C_W1Y0 = 0, MUL0, MUL0 + VEC, MUL0 + 2 * VEC
PRODUCTS = 2 * MUL0 + 2 * VEC
SUMS = ((0, 0, 1), (P, 0, 2), (PRODUCTS - P, 1, 3))
STEPS = 4
PLANES = sum(n for _, _, n in SUMS)

W_L0 = 0
W_L1 = W_L0 + 2 * MUL0
W_F1 = W_L1 + 2 * VEC
W_F2 = W_F1 + N_RADIAL
W_OA = W_F2 + W_NUMEL
W_OB = W_OA + FEAT
W_OC = W_OB + FEAT
W_OD = W_OC + FEAT
W_ALL = W_OD + FEAT

RELU_GAIN = float(np.sqrt(2.0))
MSG = 1.0 / np.sqrt(N_RADIAL) / np.sqrt(16.0)
OUT = 0.5 / np.sqrt(MUL0 + MUL1)
EPS = 1e-5


def gnn(nc, x0t, x1t, xr, ar, src, dst, edge4, basis_t, si0, si1, l10, l11, l200, l210, l201, l211,
        fc1, fc2, out):
    ctx = ExitStack()
    with ctx:
        def sb(name, shape, dt=F32):
            return ctx.enter_context(nc.sbuf_tensor(name, shape, dt))

        table = nc.dram_tensor("l_table", (NPAD, FEAT), F32).ap()

        w = sb("w", [P, W_ALL])
        a = sb("a", [P, BLOCKS])
        xres = sb("xres", [P, BLOCKS, FEAT])
        attr = sb("attr", [P, GROUPS * TILES, 4])
        rel = sb("rel", [P, GROUPS * TILES])
        base_b = sb("base_b", [P, GROUPS])
        base_i = sb("base_i", [1, GROUPS], I32)
        span_i = sb("span_i", [1, 1], I32)
        iota = sb("iota", [P, WIN])
        sums = sb("sums", [P, PLANES, NPAD])

        node_tables(nc, x0t, x1t, xr, ar, dst, edge4, si0, si1, l10, l11, l200, l210, l201, l211, fc1,
                    fc2, table, w, a, xres, attr, rel, base_b, base_i, span_i, iota, sums)

        with ExitStack() as edge_ctx:
            bufs = edge_buffers(nc, edge_ctx)
            args = (src, basis_t, table, w, attr, rel, base_i, iota, sums, bufs)
            edge_pass(nc, "first", *args)
            span = nc.values_load(span_i[0:1, 0:1], min_val=0, max_val=N_NODES)
            with nc.If(span >= WIN):
                with nc.Fori(1, PASSES) as turn:
                    with nc.If(span >= turn * WIN):
                        next_window(nc, rel, base_b, base_i)
                        edge_pass(nc, "more", *args)
                    nc.all_engine_barrier()

        finish(nc, w, a, xres, sums, out)


def node_tables(nc, x0t, x1t, xr, ar, dst, edge4, si0, si1, l10, l11, l200, l210, l201, l211, fc1, fc2,
                table, w, a, xres, attr, rel, base_b, base_i, span_i, iota, sums):
    CUT = 5
    with ExitStack() as ctx:
        def sb(name, shape, dt=F32):
            return ctx.enter_context(nc.sbuf_tensor(name, shape, dt))

        def bank(name):
            return ctx.enter_context(nc.psum_tensor(name, [P, BANK], F32))

        def sem(name):
            return ctx.enter_context(nc.semaphore(name))

        raw = sb("raw", [P, W_ALL])
        x0 = sb("x0", [MUL0, NPAD])
        x1 = sb("x1", [VEC, NPAD])
        l_sb = sb("l_sb", [P, 2, CUT, FEAT])
        dst_i = sb("dst_i", [P, GROUPS * TILES], I32)
        dst_f = sb("dst_f", [P, GROUPS * TILES])
        ext = sb("ext", [P, 2, GROUPS])
        lim = sb("lim", [GROUPS, 2])
        span = sb("span", [GROUPS, 1])
        diag = sb("diag", [GROUPS, 2, GROUPS])
        span_p = sb("span_p", [P, 1])
        eye = sb("eye", [P, P])
        ones = sb("ones", [GROUPS, P])
        node_ps = [bank(f"node_ps{i}")[:, 0:2 * FEAT].rearrange("p (k f) -> p k f", k=2) for i in range(4)]
        turn_ps = bank("turn_ps")[0:GROUPS, 0:2 * P].rearrange("g (k p) -> g k p", k=2)
        base_ps = bank("base_ps")[:, 0:2 * GROUPS].rearrange("p (k g) -> p k g", k=2)

        raw_zero = sem("raw_zero")
        raw_in = sem("raw_in")
        raw_fc = sem("raw_fc")
        raw_out = sem("raw_out")
        w_ready = sem("w_ready")
        x_in = sem("x_in")
        xr_in = sem("xr_in")
        dst_in = sem("dst_in")
        attr_in = sem("attr_in")
        node_mm = sem("node_mm")
        l_ready = sem("l_ready")
        res_ready = sem("res_ready")
        l_stored = [sem(f"l_stored{i}") for i in range(2)]
        eye_zero = sem("eye_zero")
        made = sem("made")
        const_ready = sem("const_ready")
        sums_zero = sem("sums_zero")
        found = sem("found")
        turned = sem("turned")
        spread = sem("spread")

        block = ctx.enter_context(nc.Block())
        halves = PLANES // 2

        @block.sync
        def _(sp):
            sp.dma_start(x0[:], x0t).then_inc(x_in, 16)
            sp.dma_start(x1[:], x1t).then_inc(x_in, 16)
            sp.dma_start(xres[:].rearrange("p b f -> p (b f)"), xr).then_inc(xr_in, 16)
            sp.dma_start(attr[:].rearrange("p t k -> p (t k)"), edge4).then_inc(attr_in, 16)
            rows = table.rearrange("(b p) f -> p b f", p=P)
            for c in range(BLOCKS // CUT):
                sp.wait_ge(l_ready, (c + 1) * CUT)
                sp.dma_start(rows[:, c * CUT:(c + 1) * CUT, :], l_sb[:, c % 2]).then_inc(l_stored[c % 2], 16)
            sp.wait_ge(l_stored[0], 16 * 3)
            sp.wait_ge(l_stored[1], 16 * 2)
            sp.wait_ge(attr_in, 16)

        @block.scalar
        def _(act):
            act.dma_start(dst_i[:], dst).then_inc(dst_in, 16)
            act.dma_start(a[:], ar).then_inc(xr_in, 16)
            act.wait_ge(raw_zero, 1)
            act.dma_start(raw[0:MUL0, W_L0:W_L0 + MUL0], l10).then_inc(raw_in, 16)
            act.dma_start(raw[0:MUL0, W_L0 + MUL0:W_L1], si0).then_inc(raw_in, 16)
            for d in range(DIMS):
                r = slice(d * MUL1, (d + 1) * MUL1)
                act.dma_start(raw[r, W_L1 + d * MUL1:W_L1 + (d + 1) * MUL1], l11).then_inc(raw_in, 16)
                act.dma_start(raw[r, W_L1 + VEC + d * MUL1:W_L1 + VEC + (d + 1) * MUL1], si1).then_inc(raw_in, 16)
            act.dma_start(raw[0:N_BASIS, W_F1:W_F2], fc1).then_inc(raw_fc, 16)
            act.dma_start(raw[0:N_RADIAL, W_F2:W_OA], fc2).then_inc(raw_fc, 16)
            act.wait_ge(xr_in, 32)
            for b in range(BLOCKS):
                act.wait_ge(node_mm, b + 1)
                if b % CUT == 0 and b >= 2 * CUT:
                    act.wait_ge(l_stored[(b // CUT) % 2], 16 * (b // CUT // 2))
                act.activation(l_sb[:, (b // CUT) % 2, b % CUT, :], node_ps[b % 4][:, 0, :], ACT.Copy,
                               scale=a[:, b:b + 1]).then_inc(l_ready, 1)

        @block.gpsimd
        def _(pool):
            pool.memset(eye[:], 0.0).then_inc(eye_zero, 1)
            pool.iota(iota[:], [[1, WIN]], base=0, channel_multiplier=0,
                      allow_small_or_imprecise_dtypes=True).then_inc(const_ready, 1)
            pool.wait_ge(eye_zero, 1)
            pool.affine_select(out=eye[:], in_=eye[:], compare_op=ALU.not_equal, fill=1.0, base=0,
                               pattern=[[-1, P]], channel_multiplier=1).then_inc(const_ready, 1)
            pool.memset(ones[:], 1.0).then_inc(const_ready, 1)
            pool.wait_ge(raw_zero, 1)
            sc0, vec0, vec1, vec2 = 0, MUL0, MUL0 + MUL1, MUL0 + 2 * MUL1
            for row, n, col, mat in (
                    (0, MUL0, W_OA + sc0, l200), (MUL0, MUL1, W_OA + vec0, l211),
                    (MUL0 + MUL1, MUL1, W_OA + vec1, l211),
                    (0, MUL1, W_OB + vec2, l211), (MUL1, MUL1, W_OB + sc0, l210), (MUL0, MUL0, W_OB + vec0, l201),
                    (0, MUL1, W_OC + sc0, l210), (MUL1, MUL1, W_OC + sc0, l210), (MUL0, MUL0, W_OC + vec1, l201),
                    (MUL0, MUL0, W_OD + vec2, l201)):
                pool.dma_start(raw[row:row + n, col:col + mat.shape[1]], mat).then_inc(raw_out, 16)
            pool.memset(sums[:, halves:], 0.0).then_inc(sums_zero, 1)

        @block.tensor
        def _(pe):
            pe.wait_ge(const_ready, 3)
            pe.wait_ge(found, 2)
            pe.matmul(turn_ps[:, 0, :], ext[:, 0, :], eye[:], start=True, stop=True)
            pe.matmul(turn_ps[:, 1, :], ext[:, 1, :], eye[:], start=True, stop=True).then_inc(turned, 1)

            pe.wait_ge(w_ready, 2)
            pe.wait_ge(x_in, 32)
            for b in range(BLOCKS):
                if b >= 4:
                    pe.wait_ge(l_ready, b - 3)
                    pe.wait_ge(res_ready, b - 3)
                n = slice(b * P, (b + 1) * P)
                pe.matmul(node_ps[b % 4][:, :, 0:MUL0], x0[:, n],
                          w[0:MUL0, W_L0:W_L1].rearrange("p (k f) -> p k f", k=2), start=True, stop=True)
                pe.matmul(node_ps[b % 4][:, :, MUL0:FEAT], x1[:, n],
                          w[0:VEC, W_L1:W_F1].rearrange("p (k f) -> p k f", k=2), start=True,
                          stop=True).then_inc(node_mm, 1)
                if b == 3:
                    pe.wait_ge(found, 6)
                    pe.matmul(base_ps[:, 0, :], ones[:], diag[:, 0, :], start=True, stop=True)
                    pe.matmul(base_ps[:, 1, :], ones[:], diag[:, 1, :], start=True, stop=True).then_inc(spread, 1)

        @block.vector
        def _(dve):
            dve.memset(raw[:], 0.0).then_inc(raw_zero, 1)
            dve.wait_ge(dst_in, 16)
            dve.tensor_copy(dst_f[:], dst_i[:]).then_inc(made, 1)
            dve.wait_ge(made, 1)
            by_group = dst_f[:].rearrange("p (g t) -> p g t", t=TILES)
            dve.tensor_reduce(ext[:, 0, :], by_group, AX.X, ALU.min).then_inc(found, 1)
            dve.tensor_reduce(ext[:, 1, :], by_group, AX.X, ALU.max).then_inc(found, 1)
            dve.wait_ge(raw_in, 16 * 8)
            dve.tensor_scalar(w[:, W_L0:W_L1], raw[:, W_L0:W_L1], 1.0 / float(np.sqrt(MUL0)), None,
                              ALU.mult).then_inc(w_ready, 1)
            dve.tensor_scalar(w[:, W_L1:W_F1], raw[:, W_L1:W_F1], 1.0 / float(np.sqrt(MUL1)), None,
                              ALU.mult).then_inc(w_ready, 1)
            dve.wait_ge(turned, 1)
            dve.tensor_reduce(lim[:, 0:1], turn_ps[:, 0, :], AX.X, ALU.min).then_inc(found, 1)
            dve.tensor_reduce(lim[:, 1:2], turn_ps[:, 1, :], AX.X, ALU.max).then_inc(found, 1)
            dve.wait_ge(found, 4)
            dve.tensor_tensor(span[:], lim[:, 1:2], lim[:, 0:1], ALU.subtract).then_inc(made, 1)
            dve.wait_ge(made, 2)
            dve.tensor_scalar(diag[:, 0, :], eye[0:GROUPS, 0:GROUPS], lim[:, 0:1], None, ALU.mult).then_inc(found, 1)
            dve.tensor_scalar(diag[:, 1, :], eye[0:GROUPS, 0:GROUPS], span[:], None, ALU.mult).then_inc(found, 1)
            dve.wait_ge(xr_in, 32)
            for b in range(BLOCKS):
                dve.wait_ge(l_ready, b + 1)
                dve.scalar_tensor_tensor(out=xres[:, b, :], in0=node_ps[b % 4][:, 1, :], scalar=a[:, b:b + 1],
                                         in1=xres[:, b, :], op0=ALU.mult, op1=ALU.add).then_inc(res_ready, 1)
            dve.wait_ge(spread, 1)
            dve.tensor_copy(base_b[:], base_ps[:, 0, :]).then_inc(made, 1)
            dve.tensor_copy(base_i[:], base_ps[0:1, 0, :]).then_inc(made, 1)
            dve.tensor_reduce(span_p[:], base_ps[:, 1, :], AX.X, ALU.max).then_inc(made, 1)
            dve.wait_ge(made, 5)
            dve.tensor_copy(span_i[:], span_p[0:1, :]).then_inc(made, 1)
            dve.tensor_tensor(rel[:].rearrange("p (g t) -> p g t", t=TILES), by_group,
                              base_b[:].unsqueeze(2).broadcast_to([P, GROUPS, TILES]),
                              ALU.subtract).then_inc(made, 1)
            dve.wait_ge(raw_fc, 16 * 2)
            dve.wait_ge(raw_out, 16 * 10)
            dve.tensor_copy(w[:, W_F1:W_F2], raw[:, W_F1:W_F2])
            dve.tensor_scalar(w[:, W_F2:W_OA - MUL1], raw[:, W_F2:W_OA - MUL1], float(MSG), None, ALU.mult)
            dve.tensor_scalar(w[:, W_OA - MUL1:W_OA], raw[:, W_OA - MUL1:W_OA], float(MSG / np.sqrt(3.0)), None,
                              ALU.mult)
            dve.tensor_scalar(w[:, W_OA:W_ALL], raw[:, W_OA:W_ALL], float(OUT), None, ALU.mult)
            dve.memset(sums[:, 0:halves], 0.0).then_inc(sums_zero, 1)
            dve.wait_ge(sums_zero, 2)
            dve.wait_ge(made, 7)


def next_window(nc, rel, base_b, base_i):
    with ExitStack() as ctx:
        moved = ctx.enter_context(nc.semaphore("moved"))
        block = ctx.enter_context(nc.Block())

        @block.vector
        def _(dve):
            dve.sem_clear(moved)
            dve.tensor_scalar(rel[:], rel[:], -float(WIN), None, ALU.add).then_inc(moved, 1)
            dve.tensor_scalar(base_b[:], base_b[:], float(WIN), float(LAST_WIN), ALU.add, ALU.min).then_inc(moved, 1)
            dve.wait_ge(moved, 2)
            dve.tensor_copy(base_i[:], base_b[0:1, :]).then_inc(moved, 1)
            dve.wait_ge(moved, 3)


def edge_buffers(nc, ctx):
    def sb(name, shape, dt=F32):
        return ctx.enter_context(nc.sbuf_tensor(name, shape, dt))

    def pb(name, shape):
        return ctx.enter_context(nc.psum_tensor(name, shape, F32))

    return {
        "idx": sb("idx", [P, SLOTS, TILES], I32),
        "basis": sb("basis", [P, SLOTS, GROUP]),
        "y": sb("y", [P, SLOTS, TILES, FEAT]),
        "h": sb("h", [N_RADIAL, 2, TILES, P]),
        "prod": sb("prod", [P, 2, TILES, PRODUCTS]),
        "hot": sb("hot", [P, 2, TILES, WIN]),
        "sel": sb("sel", [P, 2, TILES, 4, WIN]),
        "h_ps": pb("h_ps", [P, 2, GROUP]),
        "w_ps": pb("w_ps", [P, 2, TILES, BANK // 2]),
        "s_ps": pb("s_ps", [P, 2, BANK]),
    }


def edge_pass(nc, name, src, basis_t, table, w, attr, rel, base_i, iota, sums, bufs):
    idx, basis, y, h, prod, hot, sel = (bufs[k] for k in ("idx", "basis", "y", "h", "prod", "hot", "sel"))
    h_ps, w_ps, s_ps = (bufs[k] for k in ("h_ps", "w_ps", "s_ps"))
    with ExitStack() as ctx:
        def sem(what):
            return ctx.enter_context(nc.semaphore(f"{name}_{what}"))

        idx_in = [sem(f"idx_in{s}") for s in range(SLOTS)]
        basis_in = [sem(f"basis_in{s}") for s in range(SLOTS)]
        y_in = [sem(f"y_in{s}") for s in range(SLOTS)]
        gather_turn = sem("gather_turn")
        zeroed = sem("zeroed")
        h_made = sem("h_made")
        h_ready = sem("h_ready")
        w_made = sem("w_made")
        hot_ready = sem("hot_ready")
        sel_ready = sem("sel_ready")
        prod_ready = sem("prod_ready")
        s_made = sem("s_made")
        s_added = sem("s_added")
        all_sems = [*idx_in, *basis_in, *y_in, gather_turn, zeroed, h_made, h_ready, w_made, hot_ready, sel_ready,
                    prod_ready, s_made, s_added]
        if name != "first":
            low = min(s.num for s in all_sems)
            assert max(s.num for s in all_sems) - low == len(all_sems) - 1
            nc.gpsimd.sem_clear(range(low, low + len(all_sems)))
            nc.all_engine_barrier()

        block = ctx.enter_context(nc.Block())

        @block.sync
        def _(sp):
            def load(i, s, first):
                if not first:
                    sp.wait_ge(y_in[s], (i - s) * (16 * TILES // SLOTS))
                sp.dma_start(idx[:, s, :], src[:, bass.ds(i * TILES, TILES)]).then_inc(idx_in[s], 16)
                if first:
                    sp.wait_ge(zeroed, 1)
                else:
                    sp.wait_ge(h_made, i - SLOTS + 1)
                sp.dma_start(basis[0:N_BASIS, s, :], basis_t[:, bass.ds(i * GROUP, GROUP)]).then_inc(basis_in[s], 16)

            for s in range(SLOTS):
                load(s, s, True)
            with sp.Fori(SLOTS, TURNS_END, SLOTS) as first:
                for s in range(SLOTS):
                    load(first + s, s, False)

        @block.gpsimd
        def _(pool):
            def gather(i, s, first):
                pool.wait_ge(idx_in[s], (i - s) * (16 // SLOTS) + 16)
                if not first:
                    pool.wait_ge(prod_ready, (i - SLOTS + 1) * STEPS)
                pool.sem_inc(gather_turn, 1)
                for t in range(TILES):
                    pool.indirect_dma_start(
                        y[:, s, t, :], None, table,
                        bass.IndirectOffsetOnAxis(ap=idx[:, s, t:t + 1], axis=0)).then_inc(y_in[s], 16)

            for s in range(SLOTS):
                gather(s, s, True)
            with pool.Fori(SLOTS, TURNS_END, SLOTS) as first:
                for s in range(SLOTS):
                    gather(first + s, s, False)

        @block.tensor
        def _(pe):
            def radial_in(i, s, b, first):
                pe.wait_ge(basis_in[s], (i - s) * (16 // SLOTS) + 16)
                if not first:
                    pe.wait_ge(h_ready, i - 1)
                pe.matmul(h_ps[0:N_RADIAL, b, :], w[:, W_F1:W_F2], basis[:, s, :], start=True,
                          stop=True).then_inc(h_made, 1)

            def radial_out(i, b, first):
                pe.wait_ge(h_ready, i + 1)
                if not first:
                    pe.wait_ge(prod_ready, (i - 1) * STEPS)
                for t in range(TILES):
                    mm = pe.matmul(w_ps[:, b, t, 0:W_NUMEL], h[:, b, t, :], w[0:N_RADIAL, W_F2:W_OA], start=True,
                                   stop=True)
                mm.then_inc(w_made, 1)

            def by_target(i, b, first):
                pe.wait_ge(sel_ready, i + 1)
                pe.wait_ge(prod_ready, (i + 1) * STEPS)
                if not first:
                    pe.wait_ge(s_added, i - 1)
                plane = 0
                for col, k, n in SUMS:
                    for t in range(TILES):
                        mm = pe.matmul(s_ps[:, b, plane * WIN:(plane + n) * WIN], prod[:, b, t, col:col + P],
                                       sel[:, b, t, k:k + n, :].rearrange("p k w -> p (k w)"), start=(t == 0),
                                       stop=(t == TILES - 1))
                    plane += n
                mm.then_inc(s_made, 1)

            pe.wait_ge(zeroed, 1)
            radial_in(0, 0, 0, True)
            radial_in(1, 1, 1, True)
            radial_out(0, 0, True)
            for s in range(SLOTS):
                radial_in(s + 2, (s + 2) % SLOTS, s % 2, False)
                radial_out(s + 1, (s + 1) % 2, s == 0)
                by_target(s, s % 2, s < 2)
            with pe.Fori(SLOTS, TURNS_END - SLOTS, SLOTS) as first:
                for s in range(SLOTS):
                    radial_in(first + (s + 2), (s + 2) % SLOTS, s % 2, False)
                    radial_out(first + (s + 1), (s + 1) % 2, False)
                    by_target(first + s, s % 2, False)
            for i in range(GROUPS - SLOTS, GROUPS):
                if i + 2 < GROUPS:
                    radial_in(i + 2, (i + 2) % SLOTS, i % 2, False)
                if i + 1 < GROUPS:
                    radial_out(i + 1, (i + 1) % 2, False)
                by_target(i, i % 2, False)

        @block.scalar
        def _(act):
            def relu(i, b, first):
                act.wait_ge(h_made, i + 1)
                if not first:
                    act.wait_ge(w_made, i - 1)
                act.activation(h[:, b].rearrange("k t e -> k (t e)"), h_ps[0:N_RADIAL, b, :], ACT.Relu,
                               scale=RELU_GAIN / float(np.sqrt(N_BASIS))).then_inc(h_ready, 1)

            for s in range(SLOTS):
                relu(s, s % 2, s < 2)
            with act.Fori(SLOTS, TURNS_END, SLOTS) as first:
                for s in range(SLOTS):
                    relu(first + s, s % 2, False)

        @block.vector
        def _(dve):
            dve.memset(basis[:], 0.0).then_inc(zeroed, 1)

            def select(i, b, first):
                if not first:
                    dve.wait_ge(s_made, i - 1)
                dve.tensor_tensor(hot[:, b], iota[:].unsqueeze(1).broadcast_to([P, TILES, WIN]),
                                  rel[:, bass.ds(i * TILES, TILES)].unsqueeze(2).broadcast_to([P, TILES, WIN]),
                                  ALU.is_equal).then_inc(hot_ready, 1)
                dve.wait_ge(hot_ready, i + 1)
                dve.tensor_tensor(sel[:, b], hot[:, b].unsqueeze(2).broadcast_to([P, TILES, 4, WIN]),
                                  attr[:, bass.ds(i * TILES, TILES), :].unsqueeze(3).broadcast_to([P, TILES, 4, WIN]),
                                  ALU.mult).then_inc(sel_ready, 1)

            def products(i, s, b):
                dve.wait_ge(w_made, i + 1)
                dve.wait_ge(y_in[s], (i - s) * (16 * TILES // SLOTS) + 16 * TILES)
                y1 = y[:, s, :, MUL0:FEAT].rearrange("p t (d u) -> p t d u", d=DIMS)
                y0 = y[:, s, :, 0:MUL0]
                for k, col in ((0, C_W0Y0), (1, C_W1Y0)):
                    dve.tensor_tensor(prod[:, b, :, col:col + MUL0], w_ps[:, b, :, k * MUL0:(k + 1) * MUL0], y0,
                                      ALU.mult).then_inc(prod_ready, 1)
                for k, col in ((0, C_W2Y1), (1, C_W3Y1)):
                    wk = w_ps[:, b, :, 2 * MUL0 + k * MUL1:2 * MUL0 + (k + 1) * MUL1]
                    dve.tensor_tensor(prod[:, b, :, col:col + VEC].rearrange("p t (d u) -> p t d u", d=DIMS),
                                      wk.unsqueeze(2).broadcast_to([P, TILES, DIMS, MUL1]), y1,
                                      ALU.mult).then_inc(prod_ready, 1)

            def add(i, b, first):
                at = dve.value_load(base_i[0:1, bass.ds(i, 1)], min_val=0, max_val=LAST_WIN)
                dve.wait_ge(s_made, i + 1)
                if not first:
                    dve.wait_ge(s_added, i)
                window = sums[:, :, bass.ds(at, WIN)]
                dve.tensor_tensor(window, window, s_ps[:, b, 0:PLANES * WIN].rearrange("p (k n) -> p k n", k=PLANES),
                                  ALU.add).then_inc(s_added, 1)

            for i in range(SLOTS):
                select(i, i % 2, i < 2)
                products(i, i, i % 2)
                if i >= 1:
                    add(i - 1, (i - 1) % 2, i == 1)
            with dve.Fori(SLOTS, TURNS_END, SLOTS) as first:
                for s in range(SLOTS):
                    select(first + s, s % 2, False)
                    products(first + s, s, s % 2)
                    add(first + (s - 1), (s - 1) % 2, False)
            add(GROUPS - 1, (GROUPS - 1) % 2, False)
            dve.wait_ge(s_added, GROUPS)


def finish(nc, w, a, xres, sums, out):
    CUT = 5
    CUTS = BLOCKS // CUT
    with ExitStack() as ctx:
        def sem(name):
            return ctx.enter_context(nc.semaphore(name))

        res = ctx.enter_context(nc.sbuf_tensor("res", [P, BLOCKS, FEAT], F32))
        normed = ctx.enter_context(nc.sbuf_tensor("normed", [P, BLOCKS, FEAT], F32))
        stats = ctx.enter_context(nc.sbuf_tensor("stats", [P, BLOCKS, 6], F32))
        mv = ctx.enter_context(nc.sbuf_tensor("mv", [P, BLOCKS, 2], F32))
        std = ctx.enter_context(nc.sbuf_tensor("std", [P, BLOCKS], F32))
        inv = ctx.enter_context(nc.sbuf_tensor("inv", [P, BLOCKS], F32))
        shift = ctx.enter_context(nc.sbuf_tensor("shift", [P, BLOCKS], F32))
        eps = ctx.enter_context(nc.sbuf_tensor("eps", [P, 1], F32))
        o_ps = [ctx.enter_context(nc.psum_tensor(f"o_ps{i}", [P, BANK], F32)) for i in range(4)]

        packed = sem("packed")
        eps_ready = sem("eps_ready")
        o_made = sem("o_made")
        res_made = sem("res_made")
        stat_made = sem("stat_made")
        mv_made = sem("mv_made")
        std_made = sem("std_made")
        inv_made = sem("inv_made")
        shift_made = sem("shift_made")
        out_made = sem("out_made")
        stored = sem("stored")
        block = ctx.enter_context(nc.Block())

        @block.scalar
        def _(act):
            for c in range(CUTS):
                n = slice(c * CUT * P, (c + 1) * CUT * P)
                act.activation(sums[MUL0:P, 1, n], sums[MUL0:P, 3, n], ACT.Copy).then_inc(packed, 1)
            act.wait_ge(eps_ready, 1)
            for c in range(CUTS):
                n = slice(c * CUT, (c + 1) * CUT)
                act.wait_ge(mv_made, (c + 1) * CUT)
                act.activation(std[:, n], mv[:, n, 1], ACT.Sqrt, bias=eps[:]).then_inc(std_made, 1)
                act.wait_ge(shift_made, c + 1)
                for b in range(c * CUT, (c + 1) * CUT):
                    act.activation(normed[:, b, :], res[:, b, :], ACT.Identity, bias=shift[:, b:b + 1],
                                   scale=inv[:, b:b + 1]).then_inc(out_made, 1)

        @block.vector
        def _(dve):
            dve.memset(eps[:], EPS).then_inc(eps_ready, 1)
            for c in range(CUTS):
                n = slice(c * CUT * P, (c + 1) * CUT * P)
                dve.tensor_copy(sums[MUL1:MUL0, 1, n], sums[MUL1:MUL0, 2, n]).then_inc(packed, 1)
                dve.tensor_copy(sums[MUL1:MUL0, 4, n], sums[MUL1:MUL0, 5, n]).then_inc(packed, 1)

            def norm(c):
                n = slice(c * CUT, (c + 1) * CUT)
                dve.wait_ge(std_made, c + 1)
                dve.reciprocal(inv[:, n], std[:, n]).then_inc(inv_made, 1)
                dve.wait_ge(inv_made, c + 1)
                dve.scalar_tensor_tensor(out=shift[:, n], in0=mv[:, n, 0], scalar=-1.0, in1=inv[:, n], op0=ALU.mult,
                                         op1=ALU.mult).then_inc(shift_made, 1)

            for c in range(CUTS):
                for b in range(c * CUT, (c + 1) * CUT):
                    dve.wait_ge(o_made, b + 1)
                    dve.scalar_tensor_tensor(out=res[:, b, :], in0=o_ps[b % 4][:, 0:FEAT], scalar=a[:, b:b + 1],
                                             in1=xres[:, b, :], op0=ALU.mult, op1=ALU.add).then_inc(res_made, 1)
                    dve.wait_ge(res_made, b + 1)
                    dve.bn_stats(stats[:, b, :], res[:, b, :]).then_inc(stat_made, 1)
                    dve.wait_ge(stat_made, b + 1)
                    dve.bn_aggr(mv[:, b, :], stats[:, b, :]).then_inc(mv_made, 1)
                if c >= 1:
                    norm(c - 1)
            norm(CUTS - 1)

        @block.tensor
        def _(pe):
            for b in range(BLOCKS):
                n = slice(b * P, (b + 1) * P)
                if b % CUT == 0:
                    pe.wait_ge(packed, 3 * CUTS)
                if b >= 4:
                    pe.wait_ge(res_made, b - 3)
                o = o_ps[b % 4][:, 0:FEAT]
                pe.matmul(o, sums[:, 1, n], w[:, W_OB:W_OC], start=True, stop=False, skip_group_check=True)
                pe.matmul(o[:, 0:P], sums[:, 0, n], w[:, W_OA:W_OA + P], start=False, stop=False,
                          skip_group_check=True)
                pe.matmul(o[:, 0:P], sums[:, 4, n], w[:, W_OC:W_OC + P], start=False, stop=False,
                          skip_group_check=True)
                pe.matmul(o[:, P:FEAT], sums[MUL0:P, 5, n], w[MUL0:P, W_OD + P:W_ALL], start=False, stop=True,
                          skip_group_check=True).then_inc(o_made, 1)

        @block.sync
        def _(sp):
            for c in range(CUTS):
                n = slice(c * CUT * FEAT, (c + 1) * CUT * FEAT)
                sp.wait_ge(out_made, (c + 1) * CUT)
                sp.dma_start(out[:, n], normed[:].rearrange("p b f -> p (b f)")[:, n]).then_inc(stored, 16)
            sp.wait_ge(stored, 16 * CUTS)


def kernel(x, src, dst, edge_attr_10, edge_attr_4, node_vec1, L0_gnn_W_si0, L0_gnn_W_si1, L0_gnn_W_l1_0,
           L0_gnn_W_l1_1, L0_gnn_W_l2_00, L0_gnn_W_l2_10, L0_gnn_W_l2_01, L0_gnn_W_l2_11, L0_gnn_W_fc1,
           L0_gnn_W_fc2):
    import concourse.bacc as bacc
    from concourse.bass_utils import run_bass_kernel_spmd as run

    x, src, dst, e10, e4, node = (np.asarray(v) for v in (x, src, dst, edge_attr_10, edge_attr_4, node_vec1))
    xp = np.zeros((NPAD, FEAT), x.dtype)
    xp[:N_NODES, :MUL0] = x[:, :MUL0]
    xp[:N_NODES, MUL0:] = x[:, MUL0:].reshape(N_NODES, MUL1, DIMS).transpose(0, 2, 1).reshape(N_NODES, VEC)
    ap = np.zeros((NPAD, 1), node.dtype)
    ap[:N_NODES] = node

    def padded(v, fill):
        tail = np.empty((EPAD - N_EDGES, *v.shape[1:]), v.dtype)
        tail[:] = fill
        return np.concatenate([v, tail])

    def tiled(v):
        v = v.reshape(GROUPS, P, TILES, -1)
        return np.ascontiguousarray(v.transpose(1, 0, 2, 3).reshape(P, -1))

    basis_t = padded(e10, 0).reshape(GROUPS, P, TILES, N_BASIS).transpose(3, 0, 2, 1)
    arrays = {
        "x0t": np.ascontiguousarray(xp[:, :MUL0].T),
        "x1t": np.ascontiguousarray(xp[:, MUL0:].T),
        "xr": np.ascontiguousarray(xp.reshape(BLOCKS, P, FEAT).transpose(1, 0, 2).reshape(P, -1)),
        "ar": np.ascontiguousarray(ap.reshape(BLOCKS, P).T),
        "src_in": tiled(padded(src, 0)),
        "dst_in_d": tiled(padded(dst, dst[-1])),
        "edge4": tiled(padded(e4, 0)),
        "basis_t": np.ascontiguousarray(basis_t.reshape(N_BASIS, EPAD)),
        "si0": np.asarray(L0_gnn_W_si0), "si1": np.asarray(L0_gnn_W_si1),
        "l10": np.asarray(L0_gnn_W_l1_0), "l11": np.asarray(L0_gnn_W_l1_1),
        "l200": np.asarray(L0_gnn_W_l2_00), "l210": np.asarray(L0_gnn_W_l2_10),
        "l201": np.asarray(L0_gnn_W_l2_01), "l211": np.asarray(L0_gnn_W_l2_11),
        "fc1": np.asarray(L0_gnn_W_fc1), "fc2": np.asarray(L0_gnn_W_fc2),
    }
    nc = bacc.Bacc("TRN2", target_bir_lowering=False, num_devices=1)
    args = [nc.dram_tensor(n, v.shape, mybir.dt.from_np(v.dtype), kind="ExternalInput").ap()
            for n, v in arrays.items()]
    out = nc.dram_tensor("normed_out", (P, BLOCKS * FEAT), F32, kind="ExternalOutput").ap()
    gnn(nc, *args, out)
    r = run(nc, [arrays], core_ids=[0]).results[0]["normed_out"]
    rows = np.asarray(r).reshape(P, BLOCKS, FEAT).transpose(1, 0, 2).reshape(NPAD, FEAT)[:N_NODES]
    y = np.empty((N_NODES, FEAT), rows.dtype)
    y[:, :MUL0] = rows[:, :MUL0]
    y[:, MUL0:] = rows[:, MUL0:].reshape(N_NODES, DIMS, MUL1).transpose(0, 2, 1).reshape(N_NODES, VEC)
    return y
```

```python
from contextlib import ExitStack

import numpy as np

import concourse.bass as bass
from concourse import mybir

F32 = mybir.dt.float32
I32 = mybir.dt.int32
ALU = mybir.AluOpType
ACT = mybir.ActivationFunctionType
AX = mybir.AxisListType

P = 128
BANK = 512
N_NODES, N_EDGES = 3125, 53125
MUL0, MUL1, DIMS = 64, 32, 3
VEC = MUL1 * DIMS
FEAT = MUL0 + VEC
N_BASIS, N_RADIAL = 10, 100
W_NUMEL = 2 * MUL0 + 2 * MUL1
BLOCKS = -(-N_NODES // P)
CUT = 5
CUTS = BLOCKS // CUT
NPAD = BLOCKS * P

TILES = 4
GROUP = TILES * P
GROUPS = -(-N_EDGES // GROUP)
EPAD = GROUPS * GROUP
SLOTS = 4
TURNS_END = GROUPS - SLOTS + 1
WIN = 40
LAST_WIN = NPAD - WIN
PASSES = -(-N_NODES // WIN)
assert GROUPS % SLOTS == 0 and LAST_WIN >= N_NODES

C_W0Y0 = 0
C_W2Y1 = C_W0Y0 + MUL0
C_W3YE = C_W2Y1 + VEC
C_W1Y0 = C_W3YE + MUL1
PRODUCTS = C_W1Y0 + MUL0
STEPS = 4
MARKS = 1 + DIMS
PLANES = 1 + MARKS
assert PRODUCTS == 2 * P

W_L0 = 0
W_L1 = W_L0 + 2 * MUL0
W_F1 = W_L1 + 2 * VEC
W_F2 = W_F1 + N_RADIAL
W_OA = W_F2 + W_NUMEL
W_OB = W_OA + P
W_OC = W_OB + FEAT
W_ALL = W_OC + 2 * MUL1

RELU_GAIN = float(np.sqrt(2.0))
MSG = 1.0 / np.sqrt(N_RADIAL) / np.sqrt(16.0)
OUT = 0.5 / np.sqrt(MUL0 + MUL1)
EPS = 1e-5


def gnn(nc, x0t, x1t, xr, ar, src, dst, e0_in, e1_in, basis_t, si0, si1, l10, l11, l200, l210, l201, l211,
        fc1, fc2, out):
    ctx = ExitStack()
    with ctx:
        def sb(name, shape, dt=F32):
            return ctx.enter_context(nc.sbuf_tensor(name, shape, dt))

        table = nc.dram_tensor("l_table", (NPAD, FEAT), F32).ap()

        w = sb("w", [P, W_ALL])
        a = sb("a", [P, BLOCKS])
        xres = sb("xres", [P, BLOCKS, FEAT])
        xin = sb("xin", [P, BLOCKS, FEAT])
        e0 = sb("e0", [P, GROUPS * TILES])
        e1 = sb("e1", [P, GROUPS * TILES, DIMS])
        rel = sb("rel", [P, GROUPS * TILES])
        base_b = sb("base_b", [P, GROUPS])
        base_i = sb("base_i", [1, GROUPS], I32)
        passes_i = sb("passes_i", [1, 1], I32)
        iota = sb("iota", [P, WIN])
        sums = sb("sums", [P, PLANES, NPAD])
        x_loaded = ctx.enter_context(nc.semaphore("x_loaded"))

        node_tables(nc, x0t, x1t, xr, xin, x_loaded, ar, dst, e0_in, e1_in, si0, si1, l10, l11, l200, l210, l201, l211, fc1, fc2,
                    table, w, a, xres, e0, e1, rel, base_b, base_i, passes_i, iota, sums)

        with ExitStack() as edge_ctx:
            bufs = edge_buffers(nc, edge_ctx)
            args = (src, basis_t, table, w, e0, e1, rel, base_i, iota, sums, bufs)
            edge_pass(nc, "first", 0, *args)
            passes = nc.values_load(passes_i[0:1, 0:1], min_val=1, max_val=PASSES)
            with nc.If(passes >= 2):
                with nc.Fori(1, passes) as turn:
                    next_window(nc, rel, base_b, base_i)
                    edge_pass(nc, "more", turn - 1, *args)
                nc.all_engine_barrier()

        finish(nc, w, a, xin, x_loaded, xres, sums, out)


def node_tables(nc, x0t, x1t, xr, xin, x_loaded, ar, dst, e0_in, e1_in, si0, si1, l10, l11, l200, l210, l201, l211, fc1, fc2,
                table, w, a, xres, e0, e1, rel, base_b, base_i, passes_i, iota, sums):
    with ExitStack() as ctx:
        def sb(name, shape, dt=F32):
            return ctx.enter_context(nc.sbuf_tensor(name, shape, dt))

        def bank(name):
            return ctx.enter_context(nc.psum_tensor(name, [P, BANK], F32))

        def sem(name):
            return ctx.enter_context(nc.semaphore(name))

        raw = sb("raw", [P, W_ALL])
        x0 = sb("x0", [P, NPAD])
        x1 = sb("x1", [P, NPAD])
        l_sb = sb("l_sb", [P, 2, CUT, FEAT])
        dst_i = sb("dst_i", [P, GROUPS * TILES], I32)
        dst_f = sb("dst_f", [P, GROUPS * TILES])
        ext = sb("ext", [P, 2, GROUPS])
        lim = sb("lim", [GROUPS, 2])
        span = sb("span", [GROUPS, 1])
        diag = sb("diag", [GROUPS, 2, GROUPS])
        span_p = sb("span_p", [P, 1])
        eye = sb("eye", [P, P])
        ones = sb("ones", [GROUPS, P])
        starts = sb("starts", [1, PASSES])
        reached = sb("reached", [1, PASSES])
        n_passes = sb("n_passes", [1, 1])
        node_ps = [bank(f"node_ps{i}")[:, 0:2 * FEAT].rearrange("p (k f) -> p k f", k=2) for i in range(6)]
        turn_ps = bank("turn_ps")[0:GROUPS, 0:2 * P].rearrange("g (k p) -> g k p", k=2)
        base_ps = bank("base_ps")[:, 0:2 * GROUPS].rearrange("p (k g) -> p k g", k=2)

        first_zero = sem("first_zero")
        raw_zero = sem("raw_zero")
        x0_zero = sem("x0_zero")
        x1_zero = sem("x1_zero")
        raw_in = sem("raw_in")
        raw_fc = sem("raw_fc")
        raw_out = sem("raw_out")
        w_ready = sem("w_ready")
        x_in = [sem(f"x_in{c}") for c in range(CUTS)]
        a_in = sem("a_in")
        dst_in = sem("dst_in")
        attr_in = sem("attr_in")
        node_mm = sem("node_mm")
        l_ready = sem("l_ready")
        res_ready = sem("res_ready")
        l_stored = [sem(f"l_stored{i}") for i in range(2)]
        eye_zero = sem("eye_zero")
        made = sem("made")
        const_ready = sem("const_ready")
        sums_zero = sem("sums_zero")
        found = sem("found")
        turned = sem("turned")
        spread = sem("spread")

        block = ctx.enter_context(nc.Block())

        @block.sync
        def _(sp):
            for c in range(CUTS):
                n = slice(c * CUT * P, (c + 1) * CUT * P)
                sp.dma_start(x0[0:MUL0, n], x0t[:, n]).then_inc(x_in[c], 16)
                sp.dma_start(x1[0:VEC, n], x1t[:, n]).then_inc(x_in[c], 16)
            sp.dma_start(e0[:], e0_in).then_inc(attr_in, 16)
            sp.dma_start(e1[:].rearrange("p t k -> p (t k)"), e1_in).then_inc(attr_in, 16)
            rows = table.rearrange("(b p) f -> p b f", p=P)
            for c in range(CUTS):
                sp.wait_ge(l_ready, (c + 1) * CUT)
                sp.dma_start(rows[:, c * CUT:(c + 1) * CUT, :], l_sb[:, c % 2]).then_inc(l_stored[c % 2], 16)
            sp.dma_start(xin[:].rearrange("p b f -> p (b f)"), xr).then_inc(x_loaded, 16)
            sp.wait_ge(attr_in, 32)
            sp.wait_ge(l_stored[0], 16 * ((CUTS + 1) // 2))
            sp.wait_ge(l_stored[1], 16 * (CUTS // 2))

        @block.scalar
        def _(act):
            act.wait_ge(first_zero, 1)
            act.dma_start(raw[0:MUL0, W_L0:W_L0 + MUL0], l10).then_inc(raw_in, 16)
            act.dma_start(raw[0:MUL0, W_L0 + MUL0:W_L1], si0).then_inc(raw_in, 16)
            for d in range(DIMS):
                r = slice(d * MUL1, (d + 1) * MUL1)
                act.dma_start(raw[r, W_L1 + d * MUL1:W_L1 + (d + 1) * MUL1], l11).then_inc(raw_in, 16)
                act.dma_start(raw[r, W_L1 + VEC + d * MUL1:W_L1 + VEC + (d + 1) * MUL1], si1).then_inc(raw_in, 16)
            act.dma_start(a[:], ar).then_inc(a_in, 16)
            act.wait_ge(raw_zero, 1)
            act.dma_start(raw[0:N_BASIS, W_F1:W_F2], fc1).then_inc(raw_fc, 16)
            act.dma_start(raw[0:N_RADIAL, W_F2:W_OA], fc2).then_inc(raw_fc, 16)
            act.wait_ge(a_in, 16)
            for b in range(BLOCKS):
                act.wait_ge(node_mm, b + 1)
                if b % CUT == 0 and b >= 2 * CUT:
                    act.wait_ge(l_stored[(b // CUT) % 2], 16 * (b // CUT // 2))
                act.activation(l_sb[:, (b // CUT) % 2, b % CUT, :], node_ps[b % 6][:, 0, :], ACT.Copy,
                               scale=a[:, b:b + 1]).then_inc(l_ready, 1)

        @block.gpsimd
        def _(pool):
            pool.dma_start(dst_i[:], dst).then_inc(dst_in, 16)
            pool.memset(x1[VEC:P, :], 0.0).then_inc(x1_zero, 1)
            pool.wait_ge(x1_zero, 1)
            pool.memset(eye[:], 0.0).then_inc(eye_zero, 1)
            pool.memset(ones[:], 1.0).then_inc(const_ready, 1)
            pool.wait_ge(eye_zero, 1)
            pool.affine_select(out=eye[:], in_=eye[:], compare_op=ALU.not_equal, fill=1.0, base=0,
                               pattern=[[-1, P]], channel_multiplier=1).then_inc(const_ready, 1)
            pool.iota(iota[:], [[1, WIN]], base=0, channel_multiplier=0,
                      allow_small_or_imprecise_dtypes=True).then_inc(const_ready, 1)
            pool.iota(starts[:], [[WIN, PASSES]], base=0, channel_multiplier=0,
                      allow_small_or_imprecise_dtypes=True).then_inc(const_ready, 1)
            pool.wait_ge(raw_zero, 1)
            for row, n, col, mat in (
                    (0, MUL0, W_OA, l200), (MUL0, MUL1, W_OA + MUL0, l211), (MUL0 + MUL1, MUL1, W_OA + P - MUL1, l211),
                    (0, MUL1, W_OB + P, l211), (MUL1, MUL1, W_OB, l210), (MUL0, MUL0, W_OB + MUL0, l201),
                    (0, MUL0, W_OC + MUL1, l201), (MUL0, MUL0, W_OC, l201)):
                pool.dma_start(raw[row:row + n, col:col + mat.shape[1]], mat).then_inc(raw_out, 16)
            pool.memset(sums[:], 0.0).then_inc(sums_zero, 1)

        @block.tensor
        def _(pe):
            pe.wait_ge(const_ready, 4)
            pe.wait_ge(found, 2)
            pe.matmul(turn_ps[:, 0, :], ext[:, 0, :], eye[:], start=True, stop=True)
            pe.matmul(turn_ps[:, 1, :], ext[:, 1, :], eye[:], start=True, stop=True).then_inc(turned, 1)

            pe.wait_ge(w_ready, 2)
            pe.wait_ge(x0_zero, 1)
            pe.wait_ge(x1_zero, 1)
            for b in range(BLOCKS):
                if b % CUT == 0:
                    pe.wait_ge(x_in[b // CUT], 32)
                if b >= 6:
                    pe.wait_ge(res_ready, b - 5)
                n = slice(b * P, (b + 1) * P)
                pe.matmul(node_ps[b % 6][:, :, 0:MUL0], x0[:, n],
                          w[:, W_L0:W_L1].rearrange("p (k f) -> p k f", k=2), start=True, stop=True)
                pe.matmul(node_ps[b % 6][:, :, MUL0:FEAT], x1[:, n],
                          w[:, W_L1:W_F1].rearrange("p (k f) -> p k f", k=2), start=True,
                          stop=True).then_inc(node_mm, 1)
                if b == 0:
                    pe.wait_ge(found, 6)
                    pe.matmul(base_ps[:, 0, :], ones[:], diag[:, 0, :], start=True, stop=True)
                    pe.matmul(base_ps[:, 1, :], ones[:], diag[:, 1, :], start=True, stop=True).then_inc(spread, 1)

        @block.vector
        def _(dve):
            dve.memset(raw[:, 0:W_F1], 0.0).then_inc(first_zero, 1)
            dve.memset(raw[:, W_F1:W_ALL], 0.0).then_inc(raw_zero, 1)
            dve.memset(x0[MUL0:P, :], 0.0).then_inc(x0_zero, 1)
            dve.wait_ge(dst_in, 16)
            dve.tensor_copy(dst_f[:], dst_i[:]).then_inc(made, 1)
            dve.wait_ge(made, 1)
            by_group = dst_f[:].rearrange("p (g t) -> p g t", t=TILES)
            dve.tensor_reduce(ext[:, 0, :], by_group, AX.X, ALU.min).then_inc(found, 1)
            dve.tensor_reduce(ext[:, 1, :], by_group, AX.X, ALU.max).then_inc(found, 1)
            dve.wait_ge(raw_in, 16 * 8)
            dve.tensor_scalar(w[:, W_L0:W_L1], raw[:, W_L0:W_L1], 1.0 / float(np.sqrt(MUL0)), None,
                              ALU.mult).then_inc(w_ready, 1)
            dve.tensor_scalar(w[:, W_L1:W_F1], raw[:, W_L1:W_F1], 1.0 / float(np.sqrt(MUL1)), None,
                              ALU.mult).then_inc(w_ready, 1)
            dve.wait_ge(turned, 1)
            dve.tensor_reduce(lim[:, 0:1], turn_ps[:, 0, :], AX.X, ALU.min).then_inc(found, 1)
            dve.tensor_reduce(lim[:, 1:2], turn_ps[:, 1, :], AX.X, ALU.max).then_inc(found, 1)
            dve.wait_ge(found, 4)
            dve.tensor_tensor(span[:], lim[:, 1:2], lim[:, 0:1], ALU.subtract).then_inc(made, 1)
            dve.wait_ge(made, 2)
            dve.tensor_scalar(diag[:, 0, :], eye[0:GROUPS, 0:GROUPS], lim[:, 0:1], None, ALU.mult).then_inc(found, 1)
            dve.tensor_scalar(diag[:, 1, :], eye[0:GROUPS, 0:GROUPS], span[:], None, ALU.mult).then_inc(found, 1)
            dve.wait_ge(spread, 1)
            dve.tensor_copy(base_b[:], base_ps[:, 0, :]).then_inc(made, 1)
            dve.tensor_copy(base_i[:], base_ps[0:1, 0, :]).then_inc(made, 1)
            dve.tensor_reduce(span_p[:], base_ps[:, 1, :], AX.X, ALU.max).then_inc(made, 1)
            dve.wait_ge(made, 5)
            dve.tensor_scalar(reached[:], starts[:], span_p[0:1, :], None, ALU.is_le).then_inc(made, 1)
            dve.tensor_tensor(rel[:].rearrange("p (g t) -> p g t", t=TILES), by_group,
                              base_b[:].unsqueeze(2).broadcast_to([P, GROUPS, TILES]),
                              ALU.subtract).then_inc(made, 1)
            dve.wait_ge(made, 7)
            dve.tensor_reduce(n_passes[:], reached[:], AX.X, ALU.add).then_inc(made, 1)
            dve.wait_ge(made, 8)
            dve.tensor_copy(passes_i[:], n_passes[:]).then_inc(made, 1)
            dve.wait_ge(a_in, 16)
            for b in range(BLOCKS):
                dve.wait_ge(l_ready, b + 1)
                dve.tensor_scalar(xres[:, b, :], node_ps[b % 6][:, 1, :], a[:, b:b + 1], None,
                                  ALU.mult).then_inc(res_ready, 1)
                if b == CUT:
                    dve.wait_ge(raw_fc, 16 * 2)
                    dve.wait_ge(raw_out, 16 * 8)
                    dve.tensor_copy(w[:, W_F1:W_F2], raw[:, W_F1:W_F2]).then_inc(w_ready, 1)
                    dve.tensor_scalar(w[:, W_F2:W_OA - MUL1], raw[:, W_F2:W_OA - MUL1], float(MSG), None,
                                      ALU.mult).then_inc(w_ready, 1)
                    dve.tensor_scalar(w[:, W_OA - MUL1:W_OA], raw[:, W_OA - MUL1:W_OA], float(MSG / np.sqrt(3.0)),
                                      None, ALU.mult).then_inc(w_ready, 1)
                    dve.tensor_scalar(w[:, W_OA:W_ALL], raw[:, W_OA:W_ALL], float(OUT), None,
                                      ALU.mult).then_inc(w_ready, 1)
            dve.wait_ge(w_ready, 6)
            dve.wait_ge(made, 9)
            dve.wait_ge(res_ready, BLOCKS)


def next_window(nc, rel, base_b, base_i):
    with ExitStack() as ctx:
        moved = ctx.enter_context(nc.semaphore("moved"))
        block = ctx.enter_context(nc.Block())

        @block.vector
        def _(dve):
            dve.sem_clear(moved)
            dve.tensor_scalar(rel[:], rel[:], -float(WIN), None, ALU.add).then_inc(moved, 1)
            dve.tensor_scalar(base_b[:], base_b[:], float(WIN), float(LAST_WIN), ALU.add, ALU.min).then_inc(moved, 1)
            dve.wait_ge(moved, 2)
            dve.tensor_copy(base_i[:], base_b[0:1, :]).then_inc(moved, 1)
            dve.wait_ge(moved, 3)


def edge_buffers(nc, ctx):
    def sb(name, shape, dt=F32):
        return ctx.enter_context(nc.sbuf_tensor(name, shape, dt))

    def pb(name, shape):
        return ctx.enter_context(nc.psum_tensor(name, shape, F32))

    return {
        "idx": sb("idx", [P, SLOTS, TILES], I32),
        "basis": sb("basis", [P, SLOTS, GROUP]),
        "y": sb("y", [P, SLOTS, TILES, FEAT]),
        "ye": sb("ye", [P, 2, TILES, FEAT]),
        "h": sb("h", [N_RADIAL, 2, TILES, P]),
        "y1e": sb("y1e", [P, 2, TILES, VEC]),
        "dot": sb("dot", [P, 2, TILES, MUL1]),
        "prod": sb("prod", [P, 2, TILES, PRODUCTS]),
        "mark": sb("mark", [P, 2, TILES, MARKS, WIN]),
        "h_ps": pb("h_ps", [P, 2, GROUP]),
        "w_ps": pb("w_ps", [P, 2, TILES, BANK // 2]),
        "s_ps": pb("s_ps", [P, 2, BANK]),
    }


def edge_pass(nc, name, done, src, basis_t, table, w, e0, e1, rel, base_i, iota, sums, bufs):
    idx, basis, y, ye, h, y1e, dot, prod, mark = (bufs[k] for k in ("idx", "basis", "y", "ye", "h", "y1e", "dot", "prod",
                                                                 "mark"))
    h_ps, w_ps, s_ps = (bufs[k] for k in ("h_ps", "w_ps", "s_ps"))
    with ExitStack() as ctx:
        def sem(what):
            return ctx.enter_context(nc.semaphore(f"{name}_{what}"))

        idx_in = [sem(f"idx_in{s}") for s in range(SLOTS)]
        basis_in = [sem(f"basis_in{s}") for s in range(SLOTS)]
        y_in = [[sem(f"y_in{s}_{t}") for t in range(TILES)] for s in range(SLOTS)]
        gather_turn = sem("gather_turn")
        zeroed = sem("zeroed")
        h_made = sem("h_made")
        h_ready = sem("h_ready")
        w_made = sem("w_made")
        ye_ready = sem("ye_ready")
        hot_ready = sem("hot_ready")
        mark_ready = sem("mark_ready")
        y1e_ready = sem("y1e_ready")
        dot_ready = sem("dot_ready")
        prod_ready = sem("prod_ready")
        s_made = sem("s_made")
        s_added = sem("s_added")
        n0 = done * GROUPS
        block = ctx.enter_context(nc.Block())

        @block.sync
        def _(sp):
            def load(i, s, first):
                if not first:
                    sp.wait_ge(ye_ready, (n0 + i - SLOTS + 1) * TILES)
                sp.dma_start(idx[:, s, :], src[:, bass.ds(i * TILES, TILES)]).then_inc(idx_in[s], 16)
                if first:
                    sp.wait_ge(zeroed, done + 1)
                else:
                    sp.wait_ge(h_made, n0 + i - SLOTS + 1)
                sp.dma_start(basis[0:N_BASIS, s, :], basis_t[:, bass.ds(i * GROUP, GROUP)]).then_inc(basis_in[s], 16)

            for s in range(SLOTS):
                load(s, s, True)
            with sp.Fori(SLOTS, TURNS_END, SLOTS) as first:
                for s in range(SLOTS):
                    load(first + s, s, False)

        @block.gpsimd
        def _(pool):
            def gather(i, s, first):
                pool.wait_ge(idx_in[s], (n0 + i - s) * (16 // SLOTS) + 16)
                if not first:
                    pool.wait_ge(prod_ready, (n0 + i - SLOTS + 1) * STEPS)
                pool.sem_inc(gather_turn, 1)
                for t in range(TILES):
                    pool.indirect_dma_start(
                        y[:, s, t, :], None, table,
                        bass.IndirectOffsetOnAxis(ap=idx[:, s, t:t + 1], axis=0)).then_inc(y_in[s][t], 16)

            for s in range(SLOTS):
                gather(s, s, True)
            with pool.Fori(SLOTS, TURNS_END, SLOTS) as first:
                for s in range(SLOTS):
                    gather(first + s, s, False)

        @block.tensor
        def _(pe):
            def radial_in(i, s, b, first):
                pe.wait_ge(basis_in[s], (n0 + i - s) * (16 // SLOTS) + 16)
                if not first:
                    pe.wait_ge(h_ready, n0 + i - 1)
                pe.matmul(h_ps[0:N_RADIAL, b, :], w[:, W_F1:W_F2], basis[:, s, :], start=True,
                          stop=True).then_inc(h_made, 1)

            def radial_out(i, b, first):
                pe.wait_ge(h_ready, n0 + i + 1)
                if not first:
                    pe.wait_ge(prod_ready, (n0 + i - 1) * STEPS)
                for t in range(TILES):
                    mm = pe.matmul(w_ps[:, b, t, 0:W_NUMEL], h[:, b, t, :], w[0:N_RADIAL, W_F2:W_OA], start=True,
                                   stop=True)
                mm.then_inc(w_made, 1)

            def by_target(i, b, first):
                pe.wait_ge(mark_ready, n0 + i + 1)
                pe.wait_ge(prod_ready, (n0 + i + 1) * STEPS)
                if not first:
                    pe.wait_ge(s_added, n0 + i - 1)
                for plane, col, n in ((0, 0, 1), (1, P, MARKS)):
                    for t in range(TILES):
                        mm = pe.matmul(s_ps[:, b, plane * WIN:(plane + n) * WIN], prod[:, b, t, col:col + P],
                                       mark[:, b, t, 0:n, :].rearrange("p k w -> p (k w)"), start=(t == 0),
                                       stop=(t == TILES - 1))
                mm.then_inc(s_made, 1)

            pe.wait_ge(zeroed, done + 1)
            radial_in(0, 0, 0, True)
            radial_in(1, 1, 1, True)
            radial_out(0, 0, True)
            for s in range(SLOTS):
                radial_in(s + 2, (s + 2) % SLOTS, s % 2, False)
                radial_out(s + 1, (s + 1) % 2, s == 0)
                by_target(s, s % 2, s < 2)
            with pe.Fori(SLOTS, TURNS_END - SLOTS, SLOTS) as first:
                for s in range(SLOTS):
                    radial_in(first + (s + 2), (s + 2) % SLOTS, s % 2, False)
                    radial_out(first + (s + 1), (s + 1) % 2, False)
                    by_target(first + s, s % 2, False)
            for i in range(GROUPS - SLOTS, GROUPS):
                if i + 2 < GROUPS:
                    radial_in(i + 2, (i + 2) % SLOTS, i % 2, False)
                if i + 1 < GROUPS:
                    radial_out(i + 1, (i + 1) % 2, False)
                by_target(i, i % 2, False)

        @block.scalar
        def _(act):
            def relu(i, b, first):
                act.wait_ge(h_made, n0 + i + 1)
                if not first:
                    act.wait_ge(w_made, n0 + i - 1)
                act.activation(h[:, b].rearrange("k t e -> k (t e)"), h_ps[0:N_RADIAL, b, :], ACT.Relu,
                               scale=RELU_GAIN / float(np.sqrt(N_BASIS))).then_inc(h_ready, 1)

            def scale_y(i, s, b, first):
                if not first:
                    act.wait_ge(prod_ready, (n0 + i - 1) * STEPS)
                for t in range(TILES):
                    act.wait_ge(y_in[s][t], (n0 + i - s) * (16 // SLOTS) + 16)
                    act.activation(ye[:, b, t, :], y[:, s, t, :], ACT.Copy,
                                   scale=e0[:, bass.ds(i * TILES + t, 1)]).then_inc(ye_ready, 1)

            relu(0, 0, True)
            for s in range(SLOTS):
                relu(s + 1, (s + 1) % 2, s == 0)
                scale_y(s, s, s % 2, s < 2)
            with act.Fori(SLOTS, TURNS_END - SLOTS, SLOTS) as first:
                for s in range(SLOTS):
                    relu(first + (s + 1), (s + 1) % 2, False)
                    scale_y(first + s, s, s % 2, False)
            for i in range(GROUPS - SLOTS, GROUPS):
                if i + 1 < GROUPS:
                    relu(i + 1, (i + 1) % 2, False)
                scale_y(i, i % SLOTS, i % 2, False)

        @block.vector
        def _(dve):
            dve.memset(basis[:], 0.0).then_inc(zeroed, 1)

            def marks(i, b, first):
                if not first:
                    dve.wait_ge(s_made, n0 + i - 1)
                dve.tensor_tensor(mark[:, b, :, 0, :], iota[:].unsqueeze(1).broadcast_to([P, TILES, WIN]),
                                  rel[:, bass.ds(i * TILES, TILES)].unsqueeze(2).broadcast_to([P, TILES, WIN]),
                                  ALU.is_equal).then_inc(hot_ready, 1)
                dve.wait_ge(hot_ready, n0 + i + 1)
                dve.tensor_tensor(mark[:, b, :, 1:MARKS, :],
                                  mark[:, b, :, 0, :].unsqueeze(2).broadcast_to([P, TILES, DIMS, WIN]),
                                  e1[:, bass.ds(i * TILES, TILES), :].unsqueeze(3).broadcast_to([P, TILES, DIMS, WIN]),
                                  ALU.mult).then_inc(mark_ready, 1)

            def dots(i, s, b):
                dve.wait_ge(ye_ready, (n0 + i + 1) * TILES)
                dve.tensor_tensor(y1e[:, b].rearrange("p t (d u) -> p t d u", d=DIMS),
                                  y[:, s, :, MUL0:FEAT].rearrange("p t (d u) -> p t d u", d=DIMS),
                                  e1[:, bass.ds(i * TILES, TILES), :].unsqueeze(3).broadcast_to([P, TILES, DIMS, MUL1]),
                                  ALU.mult).then_inc(y1e_ready, 1)
                dve.wait_ge(y1e_ready, n0 + i + 1)
                dve.tensor_reduce(dot[:, b], y1e[:, b].rearrange("p t (d u) -> p t u d", d=DIMS), AX.X,
                                  ALU.add).then_inc(dot_ready, 1)

            def products(i, s, b):
                dve.wait_ge(w_made, n0 + i + 1)
                w0, w1, w2, w3 = (w_ps[:, b, :, c:c + n] for c, n in (
                    (0, MUL0), (MUL0, MUL0), (2 * MUL0, MUL1), (2 * MUL0 + MUL1, MUL1)))
                dve.tensor_tensor(prod[:, b, :, C_W1Y0:PRODUCTS], w1, y[:, s, :, 0:MUL0],
                                  ALU.mult).then_inc(prod_ready, 1)
                dve.tensor_tensor(prod[:, b, :, C_W0Y0:C_W2Y1], w0, ye[:, b, :, 0:MUL0],
                                  ALU.mult).then_inc(prod_ready, 1)
                dve.tensor_tensor(prod[:, b, :, C_W2Y1:C_W3YE].rearrange("p t (d u) -> p t d u", d=DIMS),
                                  w2.unsqueeze(2).broadcast_to([P, TILES, DIMS, MUL1]),
                                  ye[:, b, :, MUL0:FEAT].rearrange("p t (d u) -> p t d u", d=DIMS),
                                  ALU.mult).then_inc(prod_ready, 1)
                dve.wait_ge(dot_ready, n0 + i + 1)
                dve.tensor_tensor(prod[:, b, :, C_W3YE:C_W1Y0], w3, dot[:, b], ALU.mult).then_inc(prod_ready, 1)

            def add(i, b, first):
                at = dve.value_load(base_i[0:1, bass.ds(i, 1)], min_val=0, max_val=LAST_WIN)
                dve.wait_ge(s_made, n0 + i + 1)
                if not first:
                    dve.wait_ge(s_added, n0 + i)
                window = sums[:, :, bass.ds(at, WIN)]
                dve.tensor_tensor(window, window, s_ps[:, b, 0:PLANES * WIN].rearrange("p (k n) -> p k n", k=PLANES),
                                  ALU.add).then_inc(s_added, 1)

            for i in range(SLOTS):
                marks(i, i % 2, i < 2)
                dots(i, i, i % 2)
                products(i, i, i % 2)
                if i >= 1:
                    add(i - 1, (i - 1) % 2, i == 1)
            with dve.Fori(SLOTS, TURNS_END, SLOTS) as first:
                for s in range(SLOTS):
                    marks(first + s, s % 2, False)
                    dots(first + s, s, s % 2)
                    products(first + s, s, s % 2)
                    add(first + (s - 1), (s - 1) % 2, False)
            add(GROUPS - 1, (GROUPS - 1) % 2, False)


def finish(nc, w, a, xin, x_loaded, xres, sums, out):
    with ExitStack() as ctx:
        def sem(name):
            return ctx.enter_context(nc.semaphore(name))

        def sb(name, shape):
            return ctx.enter_context(nc.sbuf_tensor(name, shape, F32))

        res = sb("res", [P, BLOCKS, FEAT])
        stats = sb("stats", [P, BLOCKS, 6])
        mv = sb("mv", [P, BLOCKS, 2])
        std = sb("std", [P, BLOCKS])
        inv = sb("inv", [P, BLOCKS])
        shift = sb("shift", [P, BLOCKS])
        eps = sb("eps", [P, 1])
        o_ps = [ctx.enter_context(nc.psum_tensor(f"o_ps{i}", [P, BANK], F32)) for i in range(8)]

        low_packed = sem("low_packed")
        high_packed = sem("high_packed")
        residual = sem("residual")
        eps_ready = sem("eps_ready")
        o_made = sem("o_made")
        res_made = sem("res_made")
        stat_made = sem("stat_made")
        mv_made = sem("mv_made")
        std_made = sem("std_made")
        inv_made = sem("inv_made")
        shift_made = sem("shift_made")
        out_made = sem("out_made")
        stored = sem("stored")
        block = ctx.enter_context(nc.Block())

        @block.scalar
        def _(act):
            for c in range(CUTS):
                n = slice(c * CUT * P, (c + 1) * CUT * P)
                act.activation(sums[0:MUL0, 3, n], sums[MUL0:P, 4, n], ACT.Copy).then_inc(low_packed, 1)
            act.wait_ge(eps_ready, 1)
            for c in range(CUTS):
                n = slice(c * CUT, (c + 1) * CUT)
                act.wait_ge(mv_made, (c + 1) * CUT)
                act.activation(std[:, n], mv[:, n, 1], ACT.Sqrt, bias=eps[:]).then_inc(std_made, 1)
                act.wait_ge(shift_made, c + 1)
                for b in range(c * CUT, (c + 1) * CUT):
                    act.activation(xin[:, b, :], res[:, b, :], ACT.Identity, bias=shift[:, b:b + 1],
                                   scale=inv[:, b:b + 1]).then_inc(out_made, 1)

        @block.gpsimd
        def _(pool):
            pool.wait_ge(x_loaded, 16)
            for c in range(CUTS):
                n = slice(c * CUT, (c + 1) * CUT)
                pool.tensor_tensor(xres[:, n, :], xres[:, n, :], xin[:, n, :], ALU.add).then_inc(residual, 1)

        @block.vector
        def _(dve):
            dve.memset(eps[:], EPS).then_inc(eps_ready, 1)
            for c in range(CUTS):
                n = slice(c * CUT * P, (c + 1) * CUT * P)
                dve.tensor_copy(sums[MUL0:P, 1, n], sums[MUL0:P, 2, n]).then_inc(high_packed, 1)

            def norm(c):
                n = slice(c * CUT, (c + 1) * CUT)
                dve.wait_ge(std_made, c + 1)
                dve.reciprocal(inv[:, n], std[:, n]).then_inc(inv_made, 1)
                dve.wait_ge(inv_made, c + 1)
                dve.scalar_tensor_tensor(out=shift[:, n], in0=mv[:, n, 0], scalar=-1.0, in1=inv[:, n], op0=ALU.mult,
                                         op1=ALU.mult).then_inc(shift_made, 1)

            for c in range(CUTS):
                dve.wait_ge(residual, c + 1)
                for b in range(c * CUT, (c + 1) * CUT):
                    dve.wait_ge(o_made, b + 1)
                    dve.scalar_tensor_tensor(out=res[:, b, :], in0=o_ps[b % 8][:, 0:FEAT], scalar=a[:, b:b + 1],
                                             in1=xres[:, b, :], op0=ALU.mult, op1=ALU.add).then_inc(res_made, 1)
                    dve.wait_ge(res_made, b + 1)
                    dve.bn_stats(stats[:, b, :], res[:, b, :]).then_inc(stat_made, 1)
                    dve.wait_ge(stat_made, b + 1)
                    dve.bn_aggr(mv[:, b, :], stats[:, b, :]).then_inc(mv_made, 1)
                if c >= 1:
                    norm(c - 1)
            norm(CUTS - 1)

        @block.tensor
        def _(pe):
            for b in range(BLOCKS):
                n = slice(b * P, (b + 1) * P)
                if b % CUT == 0:
                    pe.wait_ge(low_packed, b // CUT + 1)
                    pe.wait_ge(high_packed, b // CUT + 1)
                if b >= 8:
                    pe.wait_ge(res_made, b - 7)
                o = o_ps[b % 8]
                pe.matmul(o[:, 0:FEAT], sums[:, 1, n], w[:, W_OB:W_OC], start=True, stop=False, skip_group_check=True)
                pe.matmul(o[:, 0:P], sums[:, 0, n], w[:, W_OA:W_OB], start=False, stop=False, skip_group_check=True)
                pe.matmul(o[:, FEAT - 2 * MUL1:FEAT], sums[:, 3, n], w[:, W_OC:W_ALL], start=False, stop=True,
                          skip_group_check=True).then_inc(o_made, 1)

        @block.sync
        def _(sp):
            for c in range(CUTS):
                n = slice(c * CUT * FEAT, (c + 1) * CUT * FEAT)
                sp.wait_ge(out_made, (c + 1) * CUT)
                sp.dma_start(out[:, n], xin[:].rearrange("p b f -> p (b f)")[:, n]).then_inc(stored, 16)
            sp.wait_ge(stored, 16 * CUTS)


def kernel(x, src, dst, edge_attr_10, edge_attr_4, node_vec1, L0_gnn_W_si0, L0_gnn_W_si1, L0_gnn_W_l1_0,
           L0_gnn_W_l1_1, L0_gnn_W_l2_00, L0_gnn_W_l2_10, L0_gnn_W_l2_01, L0_gnn_W_l2_11, L0_gnn_W_fc1,
           L0_gnn_W_fc2):
    import concourse.bacc as bacc
    from concourse.bass_utils import run_bass_kernel_spmd as run

    x, src, dst, e10, e4, node = (np.asarray(v) for v in (x, src, dst, edge_attr_10, edge_attr_4, node_vec1))
    xp = np.zeros((NPAD, FEAT), x.dtype)
    xp[:N_NODES, :MUL0] = x[:, :MUL0]
    xp[:N_NODES, MUL0:] = x[:, MUL0:].reshape(N_NODES, MUL1, DIMS).transpose(0, 2, 1).reshape(N_NODES, VEC)
    ap = np.zeros((NPAD, 1), node.dtype)
    ap[:N_NODES] = node

    def padded(v, fill):
        tail = np.empty((EPAD - N_EDGES, *v.shape[1:]), v.dtype)
        tail[:] = fill
        return np.concatenate([v, tail])

    def tiled(v):
        v = v.reshape(GROUPS, P, TILES, -1)
        return np.ascontiguousarray(v.transpose(1, 0, 2, 3).reshape(P, -1))

    basis_t = padded(e10, 0).reshape(GROUPS, P, TILES, N_BASIS).transpose(3, 0, 2, 1)
    arrays = {
        "x0t": np.ascontiguousarray(xp[:, :MUL0].T),
        "x1t": np.ascontiguousarray(xp[:, MUL0:].T),
        "xr": np.ascontiguousarray(xp.reshape(BLOCKS, P, FEAT).transpose(1, 0, 2).reshape(P, -1)),
        "ar": np.ascontiguousarray(ap.reshape(BLOCKS, P).T),
        "src_in": tiled(padded(src, 0)),
        "dst_in_d": tiled(padded(dst, dst[-1])),
        "e0_in": tiled(padded(e4[:, :1], 0)),
        "e1_in": tiled(padded(e4[:, 1:], 0)),
        "basis_t": np.ascontiguousarray(basis_t.reshape(N_BASIS, EPAD)),
        "si0": np.asarray(L0_gnn_W_si0), "si1": np.asarray(L0_gnn_W_si1),
        "l10": np.asarray(L0_gnn_W_l1_0), "l11": np.asarray(L0_gnn_W_l1_1),
        "l200": np.asarray(L0_gnn_W_l2_00), "l210": np.asarray(L0_gnn_W_l2_10),
        "l201": np.asarray(L0_gnn_W_l2_01), "l211": np.asarray(L0_gnn_W_l2_11),
        "fc1": np.asarray(L0_gnn_W_fc1), "fc2": np.asarray(L0_gnn_W_fc2),
    }
    nc = bacc.Bacc("TRN2", target_bir_lowering=False, num_devices=1)
    args = [nc.dram_tensor(n, v.shape, mybir.dt.from_np(v.dtype), kind="ExternalInput").ap()
            for n, v in arrays.items()]
    out = nc.dram_tensor("normed_out", (P, BLOCKS * FEAT), F32, kind="ExternalOutput").ap()
    gnn(nc, *args, out)
    r = run(nc, [arrays], core_ids=[0]).results[0]["normed_out"]
    rows = np.asarray(r).reshape(P, BLOCKS, FEAT).transpose(1, 0, 2).reshape(NPAD, FEAT)[:N_NODES]
    y = np.empty((N_NODES, FEAT), rows.dtype)
    y[:, :MUL0] = rows[:, :MUL0]
    y[:, MUL0:] = rows[:, MUL0:].reshape(N_NODES, DIMS, MUL1).transpose(0, 2, 1).reshape(N_NODES, VEC)
    return y
```

```python
from contextlib import ExitStack

import numpy as np

import concourse.bass as bass
from concourse import mybir

F32 = mybir.dt.float32
I32 = mybir.dt.int32
ALU = mybir.AluOpType
ACT = mybir.ActivationFunctionType
AX = mybir.AxisListType

P = 128
BANK = 512
N_NODES, N_EDGES = 3125, 53125
MUL0, MUL1, DIMS = 64, 32, 3
VEC = MUL1 * DIMS
FEAT = MUL0 + VEC
N_BASIS, N_RADIAL = 10, 100
W_NUMEL = 2 * MUL0 + 2 * MUL1
BLOCKS = -(-N_NODES // P)
CUT = 5
CUTS = BLOCKS // CUT
NPAD = BLOCKS * P
EDGE_CUTS = 3
BY_VECTOR = 3
NORM_ENDS = [9, 16, 21, BLOCKS]
NORMS = list(zip([0] + NORM_ENDS[:-1], NORM_ENDS))


def by_scalar(lo, hi):
    return (hi - lo + 1) // 2

TILES = 4
GROUP = TILES * P
GROUPS = -(-N_EDGES // GROUP)
EPAD = GROUPS * GROUP
SLOTS = 4
TURNS_END = GROUPS - SLOTS + 1
WIN = 40
LAST_WIN = NPAD - WIN
PASSES = -(-N_NODES // WIN)
assert GROUPS % SLOTS == 0 and LAST_WIN >= N_NODES

C_W0Y0 = 0
C_W2Y1 = C_W0Y0 + MUL0
C_W3YE = C_W2Y1 + VEC
C_W1Y0 = C_W3YE + MUL1
PRODUCTS = C_W1Y0 + MUL0
STEPS = 4
MARKS = 1 + DIMS
PLANES = 1 + MARKS
assert PRODUCTS == 2 * P

QUAD = P // MUL1
QUADS = -(-BLOCKS // QUAD)
STORES = [(0, 2), (2, 4), (4, 5), (5, QUADS)]
WARM_UP = 7
EARLY = QUADS - 3
X_QUAD = (QUAD + 1) * P
X_ALL = (QUADS - 1) * X_QUAD + (BLOCKS - (QUADS - 1) * QUAD + 1) * P
X_CUTS = [(0, X_QUAD), (X_QUAD, 2 * X_QUAD), (2 * X_QUAD, 4 * X_QUAD), (4 * X_QUAD, X_ALL)]
X_CUT_AT = {lo // X_QUAD: c for c, (lo, hi) in enumerate(X_CUTS)}

W_LA = 0
W_LB = W_LA + P
W_A = W_LB + P
W_SA = W_A + BLOCKS
W_SB = W_SA + P
W_F1 = W_SB + P
W_F2 = W_F1 + N_RADIAL
W_OA = W_F2 + W_NUMEL
W_OB = W_OA + P
W_OC = W_OB + MUL0 + MUL1
W_ALL = W_OC + 2 * MUL1
R_S = 2 * MUL1

RELU_GAIN = float(np.sqrt(2.0))
MSG = 1.0 / np.sqrt(N_RADIAL) / np.sqrt(16.0)
OUT = 0.5 / np.sqrt(MUL0 + MUL1)
EPS = 1e-5


def gnn(nc, xt, xr, w_in_d, src, dst, attr_in_d, basis_t, out):
    ctx = ExitStack()
    with ctx:
        def sb(name, shape, dt=F32):
            return ctx.enter_context(nc.sbuf_tensor(name, shape, dt))

        table = nc.dram_tensor("l_table", (NPAD, FEAT), F32).ap()

        w = sb("w", [P, W_ALL])
        xq = sb("xq", [P, X_ALL])
        xres = sb("xres", [P, BLOCKS, FEAT])
        xin = sb("xin", [P, BLOCKS, FEAT])
        attr = sb("attr", [P, GROUPS * TILES * (1 + DIMS)])
        e0 = attr[:, 0:GROUPS * TILES]
        e1 = attr[:, GROUPS * TILES:].rearrange("p (t k) -> p t k", k=DIMS)
        rel = sb("rel", [P, GROUPS * TILES])
        base_b = sb("base_b", [P, GROUPS])
        base_i = sb("base_i", [1, GROUPS], I32)
        passes_i = sb("passes_i", [1, 1], I32)
        iota = sb("iota", [P, WIN])
        sums = sb("sums", [P, PLANES, NPAD])
        idx = sb("idx", [P, SLOTS, TILES], I32)
        basis = sb("basis", [P, SLOTS, GROUP])
        x_loaded = ctx.enter_context(nc.semaphore("x_loaded"))
        attr_in = ctx.enter_context(nc.semaphore("attr_in"))

        node_tables(nc, xt, xq, w_in_d, src, dst, attr_in_d, attr_in, basis_t, table, w, xres, attr, rel, base_b,
                    base_i, passes_i, iota, sums, idx, basis)

        with ExitStack() as edge_ctx:
            bufs = edge_buffers(nc, edge_ctx)
            args = (src, basis_t, table, w, e0, e1, rel, base_i, iota, sums, idx, basis, bufs)
            edge_pass(nc, "first", 0, (xq, xres, attr_in, xr, xin, x_loaded), *args)
            passes = nc.values_load(passes_i[0:1, 0:1], min_val=1, max_val=PASSES)
            with nc.If(passes >= 2):
                with nc.Fori(1, passes) as turn:
                    next_window(nc, rel, base_b, base_i)
                    edge_pass(nc, "more", turn - 1, None, *args)
                nc.all_engine_barrier()

        finish(nc, w, w[:, W_A:W_SA], xin, xres, sums, out)


def node_tables(nc, xt, xq, w_in_d, src, dst, attr_in_d, attr_in, basis_t, table, w, xres, attr, rel, base_b,
                base_i, passes_i, iota, sums, idx, basis):
    with ExitStack() as ctx:
        def sb(name, shape, dt=F32):
            return ctx.enter_context(nc.sbuf_tensor(name, shape, dt))

        def bank(name):
            return ctx.enter_context(nc.psum_tensor(name, [P, BANK], F32))

        def sem(name):
            return ctx.enter_context(nc.semaphore(name))

        l_sb = sb("l_sb", [P, BLOCKS, FEAT])
        dst_i = sb("dst_i", [P, GROUPS * TILES], I32)
        dst_f = sb("dst_f", [P, GROUPS * TILES])
        ext = sb("ext", [P, 2, GROUPS])
        lim = sb("lim", [GROUPS, 2])
        span = sb("span", [GROUPS, 1])
        diag = sb("diag", [GROUPS, 2, GROUPS])
        span_p = sb("span_p", [P, 1])
        eye = sb("eye", [P, P])
        ones = sb("ones", [GROUPS, P])
        starts = sb("starts", [1, PASSES])
        reached = sb("reached", [1, PASSES])
        n_passes = sb("n_passes", [1, 1])
        first_copy = sb("first_copy", [P, 2])
        most_ps = [bank(f"most_ps{i}")[:].rearrange("p (j f) -> p j f", j=QUAD) for i in range(3)]
        rest_ps = [bank(f"rest_ps{i}")[:, 0:QUAD * MUL1].rearrange("p (j f) -> p j f", j=QUAD) for i in range(3)]
        turn_ps = bank("turn_ps")[0:GROUPS, 0:2 * P].rearrange("g (k p) -> g k p", k=2)
        base_ps = bank("base_ps")[:, 0:2 * GROUPS].rearrange("p (k g) -> p k g", k=2)

        node_w_in = sem("node_w_in")
        other_w_in = sem("other_w_in")
        x_in = [sem(f"x_in{c}") for c in range(len(X_CUTS))]
        dst_in = sem("dst_in")
        slots_in = sem("slots_in")
        first_zero = sem("first_zero")
        basis_zero = sem("basis_zero")
        w_ready = sem("w_ready")
        node_mm = sem("node_mm")
        most_read = sem("most_read")
        rest_read = sem("rest_read")
        l_stored = sem("l_stored")
        eye_zero = sem("eye_zero")
        made = sem("made")
        const_ready = sem("const_ready")
        sums_zero = sem("sums_zero")
        found = sem("found")
        turned = sem("turned")
        spread = sem("spread")

        def blocks_of(k):
            return k * QUAD, min(QUAD, BLOCKS - k * QUAD)

        block = ctx.enter_context(nc.Block())

        @block.sync
        def _(sp):
            sp.dma_start(w[:, 0:W_SA], w_in_d[:, 0:W_SA]).then_inc(node_w_in, 16)
            for c, (lo, hi) in enumerate(X_CUTS):
                sp.dma_start(xq[:, lo:hi], xt[:, lo:hi]).then_inc(x_in[c], 16)
            sp.dma_start(idx[:].rearrange("p s t -> p (s t)"), src[:, 0:SLOTS * TILES]).then_inc(slots_in, 16)
            sp.wait_ge(basis_zero, 1)
            sp.dma_start(basis[0:N_BASIS].rearrange("k s e -> k (s e)"),
                         basis_t[:, 0:SLOTS * GROUP]).then_inc(slots_in, 16)
            rows = table.rearrange("(b p) f -> p b f", p=P)
            for lo, hi in STORES:
                sp.wait_ge(most_read, hi)
                sp.wait_ge(rest_read, hi)
                n = slice(lo * QUAD, min(hi * QUAD, BLOCKS))
                sp.dma_start(rows[:, n, :], l_sb[:, n, :]).then_inc(l_stored, 16)
            sp.dma_start(attr[:], attr_in_d).then_inc(attr_in, 16)
            sp.wait_ge(slots_in, 32)
            sp.wait_ge(l_stored, 16 * len(STORES))

        @block.scalar
        def _(act):
            act.dma_start(dst_i[:], dst).then_inc(dst_in, 16)
            act.wait_ge(first_zero, 1)
            act.activation(first_copy[:, 1:2], first_copy[:, 0:1], ACT.Copy)
            act.wait_ge(x_in[1], 16)
            act.dma_start(w[:, W_SA:W_ALL], w_in_d[:, W_SA:W_ALL]).then_inc(other_w_in, 16)
            act.wait_ge(node_w_in, 16)
            for r in range(QUADS + EARLY):
                first, n = blocks_of(r % QUADS)
                act.wait_ge(node_mm, r + 1)
                for j in range(n):
                    to = (l_sb if r < QUADS else xres)[:, first + j, P:FEAT]
                    evict = act.activation(to, rest_ps[r % 3][:, j, :], ACT.Copy,
                                           scale=w[:, W_A + first + j:W_A + first + j + 1])
                evict.then_inc(rest_read, 1)

        @block.gpsimd
        def _(pool):
            pool.memset(eye[:], 0.0).then_inc(eye_zero, 1)
            pool.memset(ones[:], 1.0).then_inc(const_ready, 1)
            pool.wait_ge(eye_zero, 1)
            pool.affine_select(out=eye[:], in_=eye[:], compare_op=ALU.not_equal, fill=1.0, base=0,
                               pattern=[[-1, P]], channel_multiplier=1).then_inc(const_ready, 1)
            pool.iota(iota[:], [[1, WIN]], base=0, channel_multiplier=0,
                      allow_small_or_imprecise_dtypes=True).then_inc(const_ready, 1)
            pool.iota(starts[:], [[WIN, PASSES]], base=0, channel_multiplier=0,
                      allow_small_or_imprecise_dtypes=True).then_inc(const_ready, 1)
            pool.memset(sums[:], 0.0).then_inc(sums_zero, 1)

        @block.tensor
        def _(pe):
            pe.wait_ge(const_ready, 4)
            for _ in range(WARM_UP):
                pe.matmul(base_ps[:].rearrange("p k g -> p (k g)")[:, 0:P], eye[:], eye[:], start=True, stop=True)
            pe.wait_ge(found, 2)
            pe.matmul(turn_ps[:, 0, :], ext[:, 0, :], eye[:], start=True, stop=True)
            pe.matmul(turn_ps[:, 1, :], ext[:, 1, :], eye[:], start=True, stop=True).then_inc(turned, 1)

            for r in range(QUADS + EARLY):
                k = r % QUADS
                first, n = blocks_of(k)
                if r == 0:
                    pe.wait_ge(w_ready, 2)
                if r == QUADS:
                    pe.wait_ge(w_ready, 5)
                if r in X_CUT_AT:
                    pe.wait_ge(x_in[X_CUT_AT[r]], 16)
                if r >= 3:
                    pe.wait_ge(most_read, r - 2)
                    pe.wait_ge(rest_read, r - 2)
                most, rest = (W_LA, W_LB) if r < QUADS else (W_SA, W_SB)
                at = k * X_QUAD
                for j in range(n):
                    pe.matmul(most_ps[r % 3][:, j, :], xq[:, at + j * P:at + (j + 1) * P], w[:, most:most + P],
                              start=True, stop=True)
                pe.matmul(rest_ps[r % 3].rearrange("p j f -> p (j f)"), xq[:, at + n * P:at + (n + 1) * P],
                          w[:, rest:rest + P], start=True, stop=True).then_inc(node_mm, 1)
                if r == 1:
                    pe.wait_ge(found, 6)
                    pe.matmul(base_ps[:, 0, :], ones[:], diag[:, 0, :], start=True, stop=True)
                    pe.matmul(base_ps[:, 1, :], ones[:], diag[:, 1, :], start=True, stop=True).then_inc(spread, 1)

        @block.vector
        def _(dve):
            dve.memset(first_copy[:, 0:1], 0.0).then_inc(first_zero, 1)
            dve.memset(basis[:], 0.0).then_inc(basis_zero, 1)
            def scale_weights(*parts):
                for lo, hi, by in parts:
                    dve.tensor_scalar(w[:, lo:hi], w[:, lo:hi], float(by), None, ALU.mult).then_inc(w_ready, 1)

            dve.wait_ge(node_w_in, 16)
            scale_weights((W_LA, W_LA + MUL0, 1.0 / np.sqrt(MUL0)), (W_LA + MUL0, W_A, 1.0 / np.sqrt(MUL1)))
            dve.wait_ge(dst_in, 16)
            dve.tensor_copy(dst_f[:], dst_i[:]).then_inc(made, 1)
            dve.wait_ge(made, 1)
            by_group = dst_f[:].rearrange("p (g t) -> p g t", t=TILES)
            dve.tensor_reduce(ext[:, 0, :], by_group, AX.X, ALU.min).then_inc(found, 1)
            dve.tensor_reduce(ext[:, 1, :], by_group, AX.X, ALU.max).then_inc(found, 1)
            dve.wait_ge(turned, 1)
            dve.tensor_reduce(lim[:, 0:1], turn_ps[:, 0, :], AX.X, ALU.min).then_inc(found, 1)
            dve.tensor_reduce(lim[:, 1:2], turn_ps[:, 1, :], AX.X, ALU.max).then_inc(found, 1)
            dve.wait_ge(found, 4)
            dve.tensor_tensor(span[:], lim[:, 1:2], lim[:, 0:1], ALU.subtract).then_inc(made, 1)
            dve.wait_ge(made, 2)
            dve.tensor_scalar(diag[:, 0, :], eye[0:GROUPS, 0:GROUPS], lim[:, 0:1], None, ALU.mult).then_inc(found, 1)
            dve.tensor_scalar(diag[:, 1, :], eye[0:GROUPS, 0:GROUPS], span[:], None, ALU.mult).then_inc(found, 1)
            for r in range(QUADS + EARLY):
                first, n = blocks_of(r % QUADS)
                dve.wait_ge(node_mm, r + 1)
                to = (l_sb if r < QUADS else xres)[:, first:first + n, 0:P]
                dve.tensor_tensor(to, most_ps[r % 3][:, 0:n, :],
                                  w[:, W_A + first:W_A + first + n].unsqueeze(2).broadcast_to([P, n, P]),
                                  ALU.mult).then_inc(most_read, 1)
                if r == 2:
                    dve.wait_ge(other_w_in, 16)
                    scale_weights((W_SA, W_SA + R_S, 1.0 / np.sqrt(MUL1)), (W_SA + R_S, W_SB, 1.0 / np.sqrt(MUL0)),
                                  (W_SB, W_F1, 1.0 / np.sqrt(MUL1)))
                if r == QUADS:
                    scale_weights((W_F2, W_OA - MUL1, MSG), (W_OA - MUL1, W_OA, MSG / np.sqrt(3.0)),
                                  (W_OA, W_ALL, OUT))
                if r == QUADS - 1:
                    dve.wait_ge(spread, 1)
                    dve.tensor_copy(base_b[:], base_ps[:, 0, :]).then_inc(made, 1)
                    dve.tensor_copy(base_i[:], base_ps[0:1, 0, :]).then_inc(made, 1)
                    dve.tensor_reduce(span_p[:], base_ps[:, 1, :], AX.X, ALU.max).then_inc(made, 1)
                    dve.wait_ge(made, 5)
                    dve.tensor_scalar(reached[:], starts[:], span_p[0:1, :], None, ALU.is_le).then_inc(made, 1)
                    dve.tensor_tensor(rel[:].rearrange("p (g t) -> p g t", t=TILES), by_group,
                                      base_b[:].unsqueeze(2).broadcast_to([P, GROUPS, TILES]),
                                      ALU.subtract).then_inc(made, 1)
                    dve.wait_ge(made, 7)
                    dve.tensor_reduce(n_passes[:], reached[:], AX.X, ALU.add).then_inc(made, 1)
                    dve.wait_ge(made, 8)
                    dve.tensor_copy(passes_i[:], n_passes[:]).then_inc(made, 1)
            dve.wait_ge(w_ready, 8)
            dve.wait_ge(made, 9)
            dve.wait_ge(most_read, QUADS + EARLY)


def next_window(nc, rel, base_b, base_i):
    with ExitStack() as ctx:
        moved = ctx.enter_context(nc.semaphore("moved"))
        block = ctx.enter_context(nc.Block())

        @block.vector
        def _(dve):
            dve.sem_clear(moved)
            dve.tensor_scalar(rel[:], rel[:], -float(WIN), None, ALU.add).then_inc(moved, 1)
            dve.tensor_scalar(base_b[:], base_b[:], float(WIN), float(LAST_WIN), ALU.add, ALU.min).then_inc(moved, 1)
            dve.wait_ge(moved, 2)
            dve.tensor_copy(base_i[:], base_b[0:1, :]).then_inc(moved, 1)
            dve.wait_ge(moved, 3)


def edge_buffers(nc, ctx):
    def sb(name, shape, dt=F32):
        return ctx.enter_context(nc.sbuf_tensor(name, shape, dt))

    def pb(name, shape):
        return ctx.enter_context(nc.psum_tensor(name, shape, F32))

    return {
        "y": sb("y", [P, SLOTS, TILES, FEAT]),
        "ye": sb("ye", [P, 2, TILES, FEAT]),
        "h": sb("h", [N_RADIAL, 2, TILES, P]),
        "y1e": sb("y1e", [P, 2, TILES, VEC]),
        "dot": sb("dot", [P, 2, TILES, MUL1]),
        "prod": sb("prod", [P, 2, TILES, PRODUCTS]),
        "mark": sb("mark", [P, 2, TILES, MARKS, WIN]),
        "h_ps": pb("h_ps", [P, 2, GROUP]),
        "w_ps": pb("w_ps", [P, 2, TILES, BANK // 2]),
        "s_ps": pb("s_ps", [P, 2, BANK]),
    }


def edge_pass(nc, name, done, late, src, basis_t, table, w, e0, e1, rel, base_i, iota, sums, idx, basis, bufs):
    y, ye, h, y1e, dot, prod, mark = (bufs[k] for k in ("y", "ye", "h", "y1e", "dot", "prod", "mark"))
    h_ps, w_ps, s_ps = (bufs[k] for k in ("h_ps", "w_ps", "s_ps"))
    with ExitStack() as ctx:
        def sem(what):
            return ctx.enter_context(nc.semaphore(f"{name}_{what}"))

        idx_in = [sem(f"idx_in{s}") for s in range(SLOTS)]
        basis_in = [sem(f"basis_in{s}") for s in range(SLOTS)]
        y_in = [[sem(f"y_in{s}_{t}") for t in range(TILES)] for s in range(SLOTS)]
        gather_turn = sem("gather_turn")
        h_made = sem("h_made")
        h_ready = sem("h_ready")
        w_made = sem("w_made")
        ye_ready = sem("ye_ready")
        hot_ready = sem("hot_ready")
        mark_ready = sem("mark_ready")
        y1e_ready = sem("y1e_ready")
        dot_ready = sem("dot_ready")
        prod_ready = sem("prod_ready")
        s_made = sem("s_made")
        s_added = sem("s_added")
        loaded = late is not None
        if loaded:
            xq, xres, attr_in, xr, xin, x_loaded = late
            x_added = sem("x_added")
            late_made = sem("late_made")
            late_read = sem("late_read")
            late_4, late_5, late_6 = (k * X_QUAD for k in range(EARLY, QUADS))
        head_y1e = sem("head_y1e")
        head_dot = sem("head_dot")
        head_prod = sem("head_prod")
        n0 = done * GROUPS
        HEAD = TILES - 1

        def loads_of(i, s):
            return (n0 + i - s) * (16 // SLOTS) + (0 if loaded else 16)

        block = ctx.enter_context(nc.Block())

        @block.sync
        def _(sp):
            def load(i, s, first):
                if not first:
                    sp.wait_ge(ye_ready, (n0 + i - SLOTS + 1) * TILES)
                sp.dma_start(idx[:, s, :], src[:, bass.ds(i * TILES, TILES)]).then_inc(idx_in[s], 16)
                if not first:
                    sp.wait_ge(h_made, n0 + i - SLOTS + 1)
                sp.dma_start(basis[0:N_BASIS, s, :], basis_t[:, bass.ds(i * GROUP, GROUP)]).then_inc(basis_in[s], 16)

            if not loaded:
                for s in range(SLOTS):
                    load(s, s, True)
            for s in range(SLOTS):
                load(SLOTS + s, s, False)
                if loaded:
                    n = slice(s * BLOCKS * FEAT // SLOTS, (s + 1) * BLOCKS * FEAT // SLOTS)
                    sp.dma_start(xin[:].rearrange("p b f -> p (b f)")[:, n], xr[:, n]).then_inc(x_loaded, 16)
            with sp.Fori(2 * SLOTS, TURNS_END, SLOTS) as first:
                for s in range(SLOTS):
                    load(first + s, s, False)

        @block.gpsimd
        def _(pool):
            def gather(i, s, first):
                if not (first and loaded):
                    pool.wait_ge(idx_in[s], loads_of(i, s))
                if not first:
                    pool.wait_ge(prod_ready, (n0 + i - SLOTS + 1) * STEPS)
                pool.sem_inc(gather_turn, 1)
                for t in range(TILES):
                    pool.indirect_dma_start(
                        y[:, s, t, :], None, table,
                        bass.IndirectOffsetOnAxis(ap=idx[:, s, t:t + 1], axis=0)).then_inc(y_in[s][t], 16)

            for s in range(SLOTS):
                gather(s, s, True)
            with pool.Fori(SLOTS, TURNS_END, SLOTS) as first:
                for s in range(SLOTS):
                    gather(first + s, s, False)
            if loaded:
                pool.wait_ge(x_loaded, 16 * SLOTS)
                for c in range(EDGE_CUTS):
                    n = slice(c * CUT, (c + 1) * CUT)
                    pool.tensor_tensor(xres[:, n, :], xres[:, n, :], xin[:, n, :], ALU.add).then_inc(x_added, 1)
                pool.wait_ge(x_added, EDGE_CUTS)

        @block.tensor
        def _(pe):
            def radial_in(i, s, b, first):
                if not (loaded and isinstance(i, int) and i < SLOTS):
                    pe.wait_ge(basis_in[s], loads_of(i, s))
                if not first:
                    pe.wait_ge(h_ready, n0 + i - 1)
                pe.matmul(h_ps[0:N_RADIAL, b, :], w[:, W_F1:W_F2], basis[:, s, :], start=True,
                          stop=True).then_inc(h_made, 1)

            def radial_out(i, b, first):
                pe.wait_ge(h_ready, n0 + i + 1)
                if not first:
                    pe.wait_ge(prod_ready, (n0 + i - 1) * STEPS)
                for t in range(TILES):
                    mm = pe.matmul(w_ps[:, b, t, 0:W_NUMEL], h[:, b, t, :], w[0:N_RADIAL, W_F2:W_OA], start=True,
                                   stop=True)
                mm.then_inc(w_made, 1)

            def sum_tiles(b, lo, hi):
                for plane, col, n in ((0, 0, 1), (1, P, MARKS)):
                    for t in range(lo, hi):
                        mm = pe.matmul(s_ps[:, b, plane * WIN:(plane + n) * WIN], prod[:, b, t, col:col + P],
                                       mark[:, b, t, 0:n, :].rearrange("p k w -> p (k w)"), start=(t + plane == 0),
                                       stop=(t == TILES - 1), skip_group_check=True)
                return mm

            def by_target(i, b, first):
                pe.wait_ge(mark_ready, n0 + i + 1)
                pe.wait_ge(prod_ready, (n0 + i + 1) * STEPS)
                if not first:
                    pe.wait_ge(s_added, n0 + i - 1)
                sum_tiles(b, 0, TILES).then_inc(s_made, 1)

            def late_products():
                for k, at in enumerate((late_4, late_5)):
                    pe.matmul(w_ps[:, 1, k, 0:P], xq[:, at + QUAD * P:at + X_QUAD], w[:, W_SB:W_F1], start=True,
                              stop=True)
                for k, at in enumerate((late_4, late_5)):
                    for j in range(QUAD):
                        mm = pe.matmul(s_ps[:, k, j * P:(j + 1) * P], xq[:, at + j * P:at + (j + 1) * P],
                                       w[:, W_SA:W_SB], start=True, stop=True)
                    if k == 0:
                        mm.then_inc(late_made, 1)
                pe.matmul(w_ps[:, 1, 2, 0:P], xq[:, late_6:late_6 + P], w[:, W_SA:W_SB], start=True, stop=True)
                pe.matmul(w_ps[:, 1, 2, P:FEAT], xq[:, late_6 + P:X_ALL], w[:, W_SB:W_SB + MUL1], start=True,
                          stop=True).then_inc(late_made, 1)

            if loaded:
                late_products()
            radial_in(0, 0, 0, True)
            radial_in(1, 1, 1, True)
            radial_out(0, 0, True)
            if loaded:
                pe.wait_ge(late_read, 4)
            for s in range(SLOTS):
                radial_in(s + 2, (s + 2) % SLOTS, s % 2, False)
                radial_out(s + 1, (s + 1) % 2, s == 0)
                by_target(s, s % 2, s < 2)
            with pe.Fori(SLOTS, TURNS_END - SLOTS, SLOTS) as first:
                for s in range(SLOTS):
                    radial_in(first + (s + 2), (s + 2) % SLOTS, s % 2, False)
                    radial_out(first + (s + 1), (s + 1) % 2, False)
                    by_target(first + s, s % 2, False)
            for i in range(GROUPS - SLOTS, GROUPS - 1):
                if i + 2 < GROUPS:
                    radial_in(i + 2, (i + 2) % SLOTS, i % 2, False)
                radial_out(i + 1, (i + 1) % 2, False)
                by_target(i, i % 2, False)
            i = GROUPS - 1
            pe.wait_ge(mark_ready, n0 + i + 1)
            pe.wait_ge(head_prod, (done + 1) * STEPS)
            pe.wait_ge(s_added, n0 + i - 1)
            sum_tiles(i % 2, 0, HEAD)
            pe.wait_ge(prod_ready, (n0 + i + 1) * STEPS)
            sum_tiles(i % 2, HEAD, TILES).then_inc(s_made, 1)

        @block.scalar
        def _(act):
            def relu(i, b, first):
                act.wait_ge(h_made, n0 + i + 1)
                if not first:
                    act.wait_ge(w_made, n0 + i - 1)
                act.activation(h[:, b].rearrange("k t e -> k (t e)"), h_ps[0:N_RADIAL, b, :], ACT.Relu,
                               scale=RELU_GAIN / float(np.sqrt(N_BASIS))).then_inc(h_ready, 1)

            def scale_y(i, s, b, first):
                if not first:
                    act.wait_ge(prod_ready, (n0 + i - 1) * STEPS)
                for t in range(TILES):
                    act.wait_ge(y_in[s][t], (n0 + i - s) * (16 // SLOTS) + 16)
                    act.activation(ye[:, b, t, :], y[:, s, t, :], ACT.Copy,
                                   scale=e0[:, bass.ds(i * TILES + t, 1)]).then_inc(ye_ready, 1)

            if loaded:
                act.wait_ge(attr_in, 16)
            relu(0, 0, True)
            for s in range(SLOTS):
                relu(s + 1, (s + 1) % 2, s == 0)
                scale_y(s, s, s % 2, s < 2)
            with act.Fori(SLOTS, TURNS_END - SLOTS, SLOTS) as first:
                for s in range(SLOTS):
                    relu(first + (s + 1), (s + 1) % 2, False)
                    scale_y(first + s, s, s % 2, False)
            for i in range(GROUPS - SLOTS, GROUPS):
                if i + 1 < GROUPS:
                    relu(i + 1, (i + 1) % 2, False)
                scale_y(i, i % SLOTS, i % 2, False)

        @block.vector
        def _(dve):
            def marks(i, b, first):
                if not first:
                    dve.wait_ge(s_made, n0 + i - 1)
                dve.tensor_tensor(mark[:, b, :, 0, :], iota[:].unsqueeze(1).broadcast_to([P, TILES, WIN]),
                                  rel[:, bass.ds(i * TILES, TILES)].unsqueeze(2).broadcast_to([P, TILES, WIN]),
                                  ALU.is_equal).then_inc(hot_ready, 1)
                dve.wait_ge(hot_ready, n0 + i + 1)
                dve.tensor_tensor(mark[:, b, :, 1:MARKS, :],
                                  mark[:, b, :, 0, :].unsqueeze(2).broadcast_to([P, TILES, DIMS, WIN]),
                                  e1[:, bass.ds(i * TILES, TILES), :].unsqueeze(3).broadcast_to([P, TILES, DIMS, WIN]),
                                  ALU.mult).then_inc(mark_ready, 1)

            def dots(i, s, b, lo, hi, y1e_made, dot_made, count):
                n = hi - lo
                dve.wait_ge(ye_ready, (n0 + i) * TILES + hi)
                dve.tensor_tensor(y1e[:, b, lo:hi].rearrange("p t (d u) -> p t d u", d=DIMS),
                                  y[:, s, lo:hi, MUL0:FEAT].rearrange("p t (d u) -> p t d u", d=DIMS),
                                  e1[:, bass.ds(i * TILES + lo, n), :].unsqueeze(3).broadcast_to([P, n, DIMS, MUL1]),
                                  ALU.mult).then_inc(y1e_made, 1)
                dve.wait_ge(y1e_made, count)
                dve.tensor_reduce(dot[:, b, lo:hi], y1e[:, b, lo:hi].rearrange("p t (d u) -> p t u d", d=DIMS), AX.X,
                                  ALU.add).then_inc(dot_made, 1)

            def products(i, s, b, lo, hi, dot_made, count, prod_made):
                n = hi - lo
                dve.wait_ge(w_made, n0 + i + 1)
                w0, w1, w2, w3 = (w_ps[:, b, lo:hi, c:c + m] for c, m in (
                    (0, MUL0), (MUL0, MUL0), (2 * MUL0, MUL1), (2 * MUL0 + MUL1, MUL1)))
                dve.tensor_tensor(prod[:, b, lo:hi, C_W1Y0:PRODUCTS], w1, y[:, s, lo:hi, 0:MUL0],
                                  ALU.mult).then_inc(prod_made, 1)
                dve.tensor_tensor(prod[:, b, lo:hi, C_W0Y0:C_W2Y1], w0, ye[:, b, lo:hi, 0:MUL0],
                                  ALU.mult).then_inc(prod_made, 1)
                dve.tensor_tensor(prod[:, b, lo:hi, C_W2Y1:C_W3YE].rearrange("p t (d u) -> p t d u", d=DIMS),
                                  w2.unsqueeze(2).broadcast_to([P, n, DIMS, MUL1]),
                                  ye[:, b, lo:hi, MUL0:FEAT].rearrange("p t (d u) -> p t d u", d=DIMS),
                                  ALU.mult).then_inc(prod_made, 1)
                dve.wait_ge(dot_made, count)
                dve.tensor_tensor(prod[:, b, lo:hi, C_W3YE:C_W1Y0], w3, dot[:, b, lo:hi],
                                  ALU.mult).then_inc(prod_made, 1)

            def messages(i, s, b):
                dots(i, s, b, 0, TILES, y1e_ready, dot_ready, n0 + i + 1)
                products(i, s, b, 0, TILES, dot_ready, n0 + i + 1, prod_ready)

            def add(i, b, first):
                at = dve.value_load(base_i[0:1, bass.ds(i, 1)], min_val=0, max_val=LAST_WIN)
                dve.wait_ge(s_made, n0 + i + 1)
                if not first:
                    dve.wait_ge(s_added, n0 + i)
                window = sums[:, :, bass.ds(at, WIN)]
                dve.tensor_tensor(window, window, s_ps[:, b, 0:PLANES * WIN].rearrange("p (k n) -> p k n", k=PLANES),
                                  ALU.add).then_inc(s_added, 1)

            def evict_late():
                q = EARLY * QUAD

                def scaled(to, ps, nodes, shape):
                    dve.tensor_tensor(to, ps, nodes.broadcast_to(shape), ALU.mult).then_inc(late_read, 1)

                def attr_of(lo, n):
                    return w[:, W_A + lo:W_A + lo + n].unsqueeze(2)

                dve.wait_ge(late_made, 1)
                scaled(xres[:, q:q + QUAD, 0:P], s_ps[:, 0].rearrange("p (j f) -> p j f", j=QUAD), attr_of(q, QUAD),
                       [P, QUAD, P])
                scaled(xres[:, q:q + 2 * QUAD, P:FEAT].rearrange("p (k j) f -> p k j f", k=2),
                       w_ps[:, 1, 0:2, 0:P].rearrange("p k (j f) -> p k j f", j=QUAD),
                       attr_of(q, 2 * QUAD).rearrange("p (k j) f -> p k j f", k=2), [P, 2, QUAD, MUL1])
                dve.wait_ge(late_made, 2)
                scaled(xres[:, q + QUAD:q + 2 * QUAD, 0:P], s_ps[:, 1].rearrange("p (j f) -> p j f", j=QUAD),
                       attr_of(q + QUAD, QUAD), [P, QUAD, P])
                scaled(xres[:, BLOCKS - 1:BLOCKS, :], w_ps[:, 1, 2:3, 0:FEAT], attr_of(BLOCKS - 1, 1), [P, 1, FEAT])

            if loaded:
                dve.wait_ge(attr_in, 16)
            for i in range(SLOTS):
                marks(i, i % 2, i < 2)
                if i == 0 and loaded:
                    evict_late()
                messages(i, i, i % 2)
                if i >= 1:
                    add(i - 1, (i - 1) % 2, i == 1)
            with dve.Fori(SLOTS, TURNS_END - SLOTS, SLOTS) as first:
                for s in range(SLOTS):
                    marks(first + s, s % 2, False)
                    messages(first + s, s, s % 2)
                    add(first + (s - 1), (s - 1) % 2, False)
            for i in range(GROUPS - SLOTS, GROUPS - 1):
                marks(i, i % 2, False)
                messages(i, i % SLOTS, i % 2)
                add(i - 1, (i - 1) % 2, False)
            i, s, b = GROUPS - 1, SLOTS - 1, (GROUPS - 1) % 2
            marks(i, b, False)
            dots(i, s, b, 0, HEAD, head_y1e, head_dot, done + 1)
            products(i, s, b, 0, HEAD, head_dot, done + 1, head_prod)
            add(i - 1, (i - 1) % 2, False)
            dots(i, s, b, HEAD, TILES, y1e_ready, dot_ready, n0 + i + 1)
            products(i, s, b, HEAD, TILES, dot_ready, n0 + i + 1, prod_ready)
            add(GROUPS - 1, (GROUPS - 1) % 2, False)


def finish(nc, w, a, xin, xres, sums, out):
    with ExitStack() as ctx:
        def sem(name):
            return ctx.enter_context(nc.semaphore(name))

        def sb(name, shape):
            return ctx.enter_context(nc.sbuf_tensor(name, shape, F32))

        res = sb("res", [P, BLOCKS, FEAT])
        stats = sb("stats", [P, BLOCKS, 6])
        mv = sb("mv", [P, BLOCKS, 2])
        std = sb("std", [P, BLOCKS])
        inv = sb("inv", [P, BLOCKS])
        shift = sb("shift", [P, BLOCKS])
        eps = sb("eps", [P, 1])
        root = sb("root", [P, 1])
        o_ps = [ctx.enter_context(nc.psum_tensor(f"o_ps{i}", [P, BANK], F32)) for i in range(8)]

        low_packed = sem("low_packed")
        high_packed = sem("high_packed")
        high_packed_pool = sem("high_packed_pool")
        residual = sem("residual")
        eps_ready = sem("eps_ready")
        o_made = sem("o_made")
        res_made = sem("res_made")
        stat_made = sem("stat_made")
        mv_made = sem("mv_made")
        std_made = sem("std_made")
        inv_made = sem("inv_made")
        shift_made = sem("shift_made")
        out_made = sem("out_made")
        pool_out_made = sem("pool_out_made")
        last_made = sem("last_made")
        stored = sem("stored")
        block = ctx.enter_context(nc.Block())

        @block.scalar
        def _(act):
            for c in range(CUTS):
                n = slice(c * CUT * P, (c + 1) * CUT * P)
                act.activation(sums[0:MUL0, 3, n], sums[MUL0:P, 2, n], ACT.Copy).then_inc(low_packed, 1)
            act.wait_ge(eps_ready, 1)
            act.activation(root[:], eps[:], ACT.Sqrt)
            for c, (lo, hi) in enumerate(NORMS):
                act.wait_ge(mv_made, hi)
                act.activation(std[:, lo:hi], mv[:, lo:hi, 1], ACT.Sqrt, bias=eps[:]).then_inc(std_made, 1)
                act.wait_ge(shift_made, c + 1)
                for b in range(lo, lo + by_scalar(lo, hi)):
                    act.activation(xin[:, b, :], res[:, b, :], ACT.Identity, bias=shift[:, b:b + 1],
                                   scale=inv[:, b:b + 1]).then_inc(out_made, 1)

        @block.gpsimd
        def _(pool):
            for c in range(BY_VECTOR, CUTS):
                n = slice(c * CUT * P, (c + 1) * CUT * P)
                pool.tensor_copy(sums[MUL0:P, 1, n], sums[MUL0:P, 4, n]).then_inc(high_packed_pool, 1)
            pool.wait_ge(high_packed_pool, CUTS - BY_VECTOR)
            for c in range(EDGE_CUTS, CUTS):
                n = slice(c * CUT, (c + 1) * CUT)
                pool.tensor_tensor(xres[:, n, :], xres[:, n, :], xin[:, n, :], ALU.add).then_inc(residual, 1)
            for c, (lo, hi) in enumerate(NORMS[:-1]):
                pool.wait_ge(shift_made, c + 1)
                for b in range(lo + by_scalar(lo, hi), hi):
                    pool.tensor_scalar(xin[:, b, :], res[:, b, :], inv[:, b:b + 1], shift[:, b:b + 1], ALU.mult,
                                       ALU.add).then_inc(pool_out_made, 1)

        @block.vector
        def _(dve):
            dve.memset(eps[:], EPS).then_inc(eps_ready, 1)
            for c in range(BY_VECTOR):
                n = slice(c * CUT * P, (c + 1) * CUT * P)
                dve.tensor_copy(sums[MUL0:P, 1, n], sums[MUL0:P, 4, n]).then_inc(high_packed, 1)

            def norm(c):
                lo, hi = NORMS[c]
                dve.wait_ge(std_made, c + 1)
                dve.reciprocal(inv[:, lo:hi], std[:, lo:hi]).then_inc(inv_made, 1)
                dve.wait_ge(inv_made, c + 1)
                dve.scalar_tensor_tensor(out=shift[:, lo:hi], in0=mv[:, lo:hi, 0], scalar=-1.0, in1=inv[:, lo:hi],
                                         op0=ALU.mult, op1=ALU.mult).then_inc(shift_made, 1)

            for b in range(BLOCKS + 2):
                if b < BLOCKS:
                    if b % CUT == 0 and b >= EDGE_CUTS * CUT:
                        dve.wait_ge(residual, b // CUT + 1 - EDGE_CUTS)
                    dve.wait_ge(o_made, b + 1)
                    dve.scalar_tensor_tensor(out=res[:, b, :], in0=o_ps[b % 8][:, 0:FEAT], scalar=a[:, b:b + 1],
                                             in1=xres[:, b, :], op0=ALU.mult, op1=ALU.add).then_inc(res_made, 1)
                if 1 <= b <= BLOCKS:
                    dve.wait_ge(res_made, b)
                    dve.bn_stats(stats[:, b - 1, :], res[:, b - 1, :]).then_inc(stat_made, 1)
                if b >= 2:
                    dve.wait_ge(stat_made, b - 1)
                    dve.bn_aggr(mv[:, b - 2, :], stats[:, b - 2, :]).then_inc(mv_made, 1)
                for c, (_, hi) in enumerate(NORMS[:-1]):
                    if b == hi + 2:
                        norm(c)
            norm(len(NORMS) - 1)
            dve.wait_ge(shift_made, len(NORMS))
            for b in range(NORMS[-1][0] + by_scalar(*NORMS[-1]), BLOCKS):
                dve.tensor_scalar(xin[:, b, :], res[:, b, :], inv[:, b:b + 1], shift[:, b:b + 1], ALU.mult,
                                  ALU.add).then_inc(last_made, 1)

        @block.tensor
        def _(pe):
            def product(b, plane, col, weights, start, stop):
                lo, hi = weights
                return pe.matmul(o_ps[b % 8][:, col:col + hi - lo], sums[:, plane, b * P:(b + 1) * P], w[:, lo:hi],
                                 start=start, stop=stop, skip_group_check=True)

            for b in range(CUT):
                product(b, 0, 0, (W_OA, W_OB), True, False)
            for b in range(BLOCKS):
                if b >= CUT:
                    if b >= 8:
                        pe.wait_ge(res_made, b - 7)
                    product(b, 0, 0, (W_OA, W_OB), True, False)
                if b % CUT == 0:
                    if b < BY_VECTOR * CUT:
                        pe.wait_ge(high_packed, b // CUT + 1)
                    else:
                        pe.wait_ge(high_packed_pool, b // CUT + 1 - BY_VECTOR)
                product(b, 1, R_S, (W_OB, W_OC), False, False)
                if b % CUT == 0:
                    pe.wait_ge(low_packed, b // CUT + 1)
                product(b, 3, 0, (W_OC, W_ALL), False, True).then_inc(o_made, 1)

        @block.sync
        def _(sp):
            scalars = pools = 0
            for lo, hi in NORMS:
                n = slice(lo * FEAT, hi * FEAT)
                scalars += by_scalar(lo, hi)
                sp.wait_ge(out_made, scalars)
                if hi < BLOCKS:
                    pools += hi - lo - by_scalar(lo, hi)
                    sp.wait_ge(pool_out_made, pools)
                else:
                    sp.wait_ge(last_made, hi - lo - by_scalar(lo, hi))
                sp.dma_start(out[:, n], xin[:].rearrange("p b f -> p (b f)")[:, n]).then_inc(stored, 16)
            sp.wait_ge(stored, 16 * len(NORMS))


def kernel(x, src, dst, edge_attr_10, edge_attr_4, node_vec1, L0_gnn_W_si0, L0_gnn_W_si1, L0_gnn_W_l1_0,
           L0_gnn_W_l1_1, L0_gnn_W_l2_00, L0_gnn_W_l2_10, L0_gnn_W_l2_01, L0_gnn_W_l2_11, L0_gnn_W_fc1,
           L0_gnn_W_fc2):
    import concourse.bacc as bacc
    from concourse.bass_utils import run_bass_kernel_spmd as run

    x, src, dst, e10, e4, node = (np.asarray(v) for v in (x, src, dst, edge_attr_10, edge_attr_4, node_vec1))
    xp = np.zeros((NPAD, FEAT), x.dtype)
    xp[:N_NODES, :MUL0] = x[:, :MUL0]
    xp[:N_NODES, MUL0:] = x[:, MUL0:].reshape(N_NODES, MUL1, DIMS).transpose(0, 2, 1).reshape(N_NODES, VEC)
    ap = np.zeros((NPAD, 1), node.dtype)
    ap[:N_NODES] = node
    order = np.concatenate([np.arange(MUL0, P), np.arange(MUL0), np.arange(P, FEAT)])
    xt = np.zeros((P, X_ALL), x.dtype)
    for k in range(QUADS):
        blocks = range(k * QUAD, min((k + 1) * QUAD, BLOCKS))
        rest = k * X_QUAD + len(blocks) * P
        for j, b in enumerate(blocks):
            rows = xp[b * P:(b + 1) * P].T
            xt[:, k * X_QUAD + j * P:k * X_QUAD + (j + 1) * P] = rows[:P]
            xt[j * MUL1:(j + 1) * MUL1, rest:rest + P] = rows[P:]
    ww = np.zeros((P, W_ALL), x.dtype)

    def put(row, col, mat):
        mat = np.asarray(mat)
        ww[row:row + mat.shape[0], col:col + mat.shape[1]] = mat

    for most, rest, scalars, vectors, w_0, w_1 in (
            (W_LA, W_LB, 0, MUL0, L0_gnn_W_l1_0, L0_gnn_W_l1_1), (W_SA, W_SB, R_S, 0, L0_gnn_W_si0, L0_gnn_W_si1)):
        put(0, most + scalars, w_0)
        for d in range(2):
            put(MUL0 + d * MUL1, most + vectors + d * MUL1, w_1)
        for j in range(QUAD):
            put(j * MUL1, rest + j * MUL1, w_1)
    put(0, W_A, ap.reshape(BLOCKS, P).T)
    put(0, W_F1, L0_gnn_W_fc1)
    put(0, W_F2, L0_gnn_W_fc2)
    for row, col, mat in ((0, W_OA + R_S, L0_gnn_W_l2_00), (MUL0, W_OA, L0_gnn_W_l2_11),
                          (MUL0 + MUL1, W_OA + MUL1, L0_gnn_W_l2_11), (0, W_OB + MUL0, L0_gnn_W_l2_11),
                          (MUL1, W_OB, L0_gnn_W_l2_10), (MUL0, W_OB + MUL0, L0_gnn_W_l2_01),
                          (0, W_OC, L0_gnn_W_l2_01), (MUL0, W_OC + MUL1, L0_gnn_W_l2_01)):
        put(row, col, mat)

    def padded(v, fill):
        tail = np.empty((EPAD - N_EDGES, *v.shape[1:]), v.dtype)
        tail[:] = fill
        return np.concatenate([v, tail])

    def tiled(v):
        v = v.reshape(GROUPS, P, TILES, -1)
        return np.ascontiguousarray(v.transpose(1, 0, 2, 3).reshape(P, -1))

    basis_t = padded(e10, 0).reshape(GROUPS, P, TILES, N_BASIS).transpose(3, 0, 2, 1)
    arrays = {
        "xt": xt,
        "xr": np.ascontiguousarray(xp[:, order].reshape(BLOCKS, P, FEAT).transpose(1, 0, 2).reshape(P, -1)),
        "ww": ww,
        "src_in": tiled(padded(src, 0)),
        "dst_in_d": tiled(padded(dst, dst[-1])),
        "attr_in": np.concatenate([tiled(padded(e4[:, :1], 0)), tiled(padded(e4[:, 1:], 0))], 1),
        "basis_t": np.ascontiguousarray(basis_t.reshape(N_BASIS, EPAD)),
    }
    nc = bacc.Bacc("TRN2", target_bir_lowering=False, num_devices=1)
    args = [nc.dram_tensor(n, v.shape, mybir.dt.from_np(v.dtype), kind="ExternalInput").ap()
            for n, v in arrays.items()]
    out = nc.dram_tensor("normed_out", (P, BLOCKS * FEAT), F32, kind="ExternalOutput").ap()
    gnn(nc, *args, out)
    r = run(nc, [arrays], core_ids=[0]).results[0]["normed_out"]
    rows = np.asarray(r).reshape(P, BLOCKS, FEAT).transpose(1, 0, 2).reshape(NPAD, FEAT)[:N_NODES]
    rows = rows[:, np.argsort(order)]
    y = np.empty((N_NODES, FEAT), rows.dtype)
    y[:, :MUL0] = rows[:, :MUL0]
    y[:, MUL0:] = rows[:, MUL0:].reshape(N_NODES, DIMS, MUL1).transpose(0, 2, 1).reshape(N_NODES, VEC)
    return y
```
